# Optimizing a Trainium2 kernel written in Bass

```python
import numpy as np
import jax
import jax.numpy as jnp

def _softmax(x, axis=-1):
    return jax.nn.softmax(x, axis=axis)

def _gelu(x):
    return jax.nn.gelu(x, approximate=True)

def _silu(x):
    return jax.nn.silu(x)

def _sigmoid(x):
    return jax.nn.sigmoid(x)

def _layernorm(x, axis=-1, eps=1e-05):
    m = jnp.mean(x, axis=axis, keepdims=True)
    v = jnp.var(x, axis=axis, keepdims=True)
    return (x - m) / jnp.sqrt(v + eps)

def _scatter_add(tgt, idx, src, axis=0):
    return tgt.at[idx].add(src)

def _segment_sum(src, seg, n):
    return jax.ops.segment_sum(src, seg, n)
kernel_name = 'mk_seq_postln_d1_jaxref_r8_341154'

def setup_inputs(seed: int=0):
    np.random.seed(seed)
    _w = jnp.asarray

    def _L0_attn_setup():
        import jax, jax.numpy as jnp
        import numpy as np
        EMBED_DIM = 128
        NUM_HEADS = 16
        HEAD_DIM = EMBED_DIM // NUM_HEADS
        key = jax.random.key(seed)
        k1, k2, k3 = jax.random.split(key, 3)
        inputs = jax.random.normal(k1, (4, 256, EMBED_DIM), dtype=jnp.float32)
        rotation_params = jax.random.normal(k2, (NUM_HEADS, HEAD_DIM), dtype=jnp.float32)
        entangle_params = jax.random.normal(k3, (NUM_HEADS, HEAD_DIM), dtype=jnp.float32)
        return {'inputs': inputs, 'rotation_params': rotation_params, 'entangle_params': entangle_params}
    _L0_attn_in = _L0_attn_setup()

    def _L0_ffn_setup():
        import jax, jax.numpy as jnp
        import numpy as np
        DIM = 128

        def _reference_tuple_inner(x, W_r, W_k, W_v, mu_r, mu_k):
            B, T, C = x.shape
            x_prev = jnp.concatenate([jnp.zeros((B, 1, C), x.dtype), x[:, :-1, :]], axis=1)
            xr = mu_r * x + (1.0 - mu_r) * x_prev
            xk = mu_k * x + (1.0 - mu_k) * x_prev
            r = jax.nn.sigmoid(jnp.einsum('btc,dc->btd', xr, W_r))
            k = jnp.einsum('btc,dc->btd', xk, W_k)
            k_act = jnp.square(jax.nn.relu(k))
            out = r * jnp.einsum('btc,dc->btd', k_act, W_v)
            new_state = x[:, -1, :]
            return (out, new_state)
        key = jax.random.key(seed)
        ks = jax.random.split(key, 6)
        B, T, C = (8, 256, DIM)
        x = jax.random.normal(ks[0], (B, T, C), dtype=jnp.float32)
        s = 1.0 / np.sqrt(C)
        W_r = jax.random.uniform(ks[1], (C, C), jnp.float32, -s, s)
        W_k = jax.random.uniform(ks[2], (C, C), jnp.float32, -s, s)
        W_v = jax.random.uniform(ks[3], (C, C), jnp.float32, -s, s)
        mu_r = jax.random.uniform(ks[4], (C,), jnp.float32)
        mu_k = jax.random.uniform(ks[5], (C,), jnp.float32)
        return {'x': x, 'W_r': W_r, 'W_k': W_k, 'W_v': W_v, 'mu_r': mu_r, 'mu_k': mu_k}
    _L0_ffn_in = _L0_ffn_setup()
    _d = {'L0_attn_inputs': _L0_attn_in['inputs'], 'L0_attn_rotation_params': _L0_attn_in['rotation_params'], 'L0_attn_entangle_params': _L0_attn_in['entangle_params'], 'L0_ffn_W_r': _L0_ffn_in['W_r'], 'L0_ffn_W_k': _L0_ffn_in['W_k'], 'L0_ffn_W_v': _L0_ffn_in['W_v'], 'L0_ffn_mu_r': _L0_ffn_in['mu_r'], 'L0_ffn_mu_k': _L0_ffn_in['mu_k']}
    _x0 = _d['L0_attn_inputs']
    _d['L0_attn_inputs'] = jax.random.normal(jax.random.fold_in(jax.random.key(seed), 1), (2, 1024, 128), dtype=_x0.dtype)
    del _x0
    return _d

def reference(L0_attn_inputs, L0_attn_rotation_params, L0_attn_entangle_params, L0_ffn_W_r, L0_ffn_W_k, L0_ffn_W_v, L0_ffn_mu_r, L0_ffn_mu_k):

    def _L0_attn_ref(inputs, rotation_params, entangle_params):
        import jax, jax.numpy as jnp
        import numpy as np
        EMBED_DIM = 128
        NUM_HEADS = 16
        HEAD_DIM = EMBED_DIM // NUM_HEADS
        B, T, _ = inputs.shape
        x = inputs.reshape(B, T, NUM_HEADS, HEAD_DIM).transpose(0, 2, 1, 3)
        q = x * rotation_params[None, :, None, :]
        k = x * entangle_params[None, :, None, :]
        v = x
        scale = 1.0 / np.sqrt(HEAD_DIM).astype(np.float32)
        attn_scores = jnp.einsum('bhid,bhjd->bhij', q, k) * scale
        attn_weights = jax.nn.softmax(attn_scores, axis=-1)
        out = jnp.einsum('bhij,bhjd->bhid', attn_weights, v)
        out = out.transpose(0, 2, 1, 3).reshape(B, T, EMBED_DIM)
        return out

    def _L0_ffn_ref(x, W_r, W_k, W_v, mu_r, mu_k):
        import jax, jax.numpy as jnp
        import numpy as np
        DIM = 128

        def _reference_tuple_inner(x, W_r, W_k, W_v, mu_r, mu_k):
            B, T, C = x.shape
            x_prev = jnp.concatenate([jnp.zeros((B, 1, C), x.dtype), x[:, :-1, :]], axis=1)
            xr = mu_r * x + (1.0 - mu_r) * x_prev
            xk = mu_k * x + (1.0 - mu_k) * x_prev
            r = jax.nn.sigmoid(jnp.einsum('btc,dc->btd', xr, W_r))
            k = jnp.einsum('btc,dc->btd', xk, W_k)
            k_act = jnp.square(jax.nn.relu(k))
            out = r * jnp.einsum('btc,dc->btd', k_act, W_v)
            new_state = x[:, -1, :]
            return (out, new_state)
        return _reference_tuple_inner(x, W_r, W_k, W_v, mu_r, mu_k)[0]
    x = L0_attn_inputs
    x = _layernorm(x + _L0_attn_ref(x, L0_attn_rotation_params, L0_attn_entangle_params), axis=-1)
    x = _layernorm(x + _L0_ffn_ref(x, L0_ffn_W_r, L0_ffn_W_k, L0_ffn_W_v, L0_ffn_mu_r, L0_ffn_mu_k), axis=-1)
    return x

_drawn_inputs = setup_inputs


def setup_inputs(seed=0):
    import zlib

    import numpy as np

    out = dict(_drawn_inputs(seed))
    spreads = {}
    factors = {'L0_ffn_W_r': 3.117, 'L0_ffn_mu_r': 6.206}
    for name, (base, spread) in spreads.items():
        noise = np.random.default_rng([zlib.crc32(name.encode()), seed]).standard_normal(out[name].shape)
        drawn = base * np.exp(spread * noise) if base else spread * noise
        out[name] = jnp.asarray(drawn.astype(out[name].dtype))
    for name, factor in factors.items():
        out[name] = (out[name] * factor).astype(out[name].dtype)
    return out
```

```python
from contextlib import ExitStack

import concourse.bass as bass
from concourse import mybir

ALU = mybir.AluOpType
ACT = mybir.ActivationFunctionType
F32 = mybir.dt.float32
BF16 = mybir.dt.bfloat16
AX = mybir.AxisListType


def build_attention_ffn(
    nc: bass.Bass,
    x_in: bass.AP,
    rotation: bass.AP,
    entangle: bass.AP,
    W_r: bass.AP,
    W_k: bass.AP,
    W_v: bass.AP,
    mu_r: bass.AP,
    mu_k: bass.AP,
    out: bass.AP,
):
    B, T, C = x_in.shape
    H, D = rotation.shape
    P = 128
    GH = 4
    GPB = H // GH
    NG = B * GPB
    GC = GH * D
    NT = T // P
    HS2 = NT // 2
    HALF = T // 2
    BANK = 512
    PARTS = 3
    TERMS = PARTS * PARTS * D
    ROWS = TERMS + PARTS
    VW = 32
    SCALE = float(D) ** -0.5
    EPS = 1e-5

    STEPS = 2 * NT
    HS = NT
    LEAD = HS + 3
    UNITS = 2
    GUNITS = UNITS * STEPS
    TURN1 = HS - 2
    TURN0 = STEPS - 2
    RING = 3
    FILLS = GH * STEPS + 2
    BUF = 3
    SLOADS = 3 * PARTS * PARTS
    MAXROWS = PARTS * 16
    TC = BANK // C
    NC = B * NT // TC

    def fill_rank(n, unit, last=False):
        turned = (1 if unit >= GH * TURN1 else 0) + (1 if unit >= GH * TURN0 and not last else 0)
        return 1 + FILLS * n + unit + turned

    def turn_rank(n, which):
        return 1 + FILLS * n + (GH * TURN1 if which else GH * TURN0 + 1)

    def slot(rank):
        return rank % RING

    with ExitStack() as ctx:
        def sb(name, shape, dt):
            return ctx.enter_context(nc.sbuf_tensor(name, shape, dt))

        def psum(name, shape, dt):
            return ctx.enter_context(nc.psum_tensor(name, shape, dt))

        def sem(name):
            return ctx.enter_context(nc.semaphore(name))

        q_parts_dram = nc.dram_tensor("q_parts", (NG, PARTS, GC, T), BF16).ap()
        k_parts_dram = nc.dram_tensor("k_parts", (NG, PARTS, GC, T), BF16).ap()

        x_sb = sb("x_sb", [P, B * NT, C], F32)
        ident = sb("ident", [P, P], F32)
        ident_bf = sb("ident_bf", [P, P], BF16)
        columns = sb("columns", [P, 4], F32)
        qk_full = sb("qk_full", [P, 2 * B, T], F32)
        qk_rest = sb("qk_rest", [P, 2 * B, T], F32)
        qk_parts = sb("qk_parts", [P, 2 * B, PARTS, T], BF16)
        q_stack = sb("q_stack", [ROWS, BUF, 2, GH, HALF], BF16)
        k_stack = sb("k_stack", [ROWS, BUF, GH, T], BF16)
        v_aug = sb("v_aug", [P, BUF, NT, GH, VW], F32)
        neg_max = sb("neg_max", [P, 2, 16], F32)
        max_rest = sb("max_rest", [P, 2, 2, 16], F32)
        max_parts = sb("max_parts", [P, 2, P // 16, 16], BF16)
        no_max = sb("no_max", [P, 16], F32)
        max_turned = sb("max_turned", [MAXROWS, 2, P], BF16)
        probs = sb("probs", [P, 2, GH, HALF], F32)
        attn_T = sb("attn_T", [P, NG, T], F32)

        recip_sum = sb("recip_sum", [P, NC, TC * H], F32)
        y_sb = sb("y_sb", [P, NC, TC, C], F32)
        h_sb = sb("h_sb", [P, NC, TC, C], F32)
        stats = sb("stats", [P, 2, NC, TC, 6], F32)
        mean_var = sb("mean_var", [P, 2, NC, TC, 2], F32)
        var_eps = sb("var_eps", [P, 2, NC, TC], F32)
        rstd = sb("rstd", [P, 2, NC, TC], F32)
        mean_rstd = sb("mean_rstd", [P, NC, TC], F32)
        neg_mean_rstd = sb("neg_mean_rstd", [P, NC, TC], F32)
        minus_half = sb("minus_half", [P, TC], F32)
        w_sb = sb("w_sb", [P, 3, C], F32)
        w_T = sb("w_T", [P, 5, C], F32)
        one_minus_mu = sb("one_minus_mu", [P, 2], F32)
        h_T = sb("h_T", [P, B, 1 + T], F32)
        by_chunk = [t[:, 2 * i:2 * i + 2, :].rearrange("p b (n f) -> p (b n) f", f=BANK)
                    for t in (qk_full, qk_rest) for i in range(2)]
        relu_k, k_act = by_chunk[0], by_chunk[1]
        gate = by_chunk[2].rearrange("p n (t c) -> p n t c", c=C)
        z_sb = by_chunk[3].rearrange("p n (t c) -> p n t c", c=C)
        o_sb = probs[:, 0, :, :].rearrange("p n (t c) -> p n t c", c=C)

        ring_ps = psum("ring_ps", [P, RING + 1, BANK], F32)
        max_ps = psum("max_ps", [P, 2, 2, BANK], F32)

        acc_ps = ring_ps[:, RING, :]

        x_landed = [sem(f"x_landed{i}") for i in range(4)]
        columns_landed = sem("columns_landed")
        w_landed = sem("w_landed")
        ident_steps = sem("ident_steps")
        ident_set = sem("ident_set")
        pool_ones_set = sem("pool_ones_set")
        ones_set = sem("ones_set")
        v_cleared = sem("v_cleared")
        x_turned = sem("x_turned")
        qk_scaled = sem("qk_scaled")
        dve_split = sem("dve_split")
        pool_split = sem("pool_split")
        parts_stored = [sem(f"parts_stored{i}") for i in range(3)]
        stack_landed = [sem(f"stack_landed{i}") for i in range(BUF)]
        max_row_landed = [sem(f"max_row_landed{i}") for i in range(2)]
        rows_ready = sem("rows_ready")
        max_taken = sem("max_taken")
        max_split = sem("max_split")
        v_staged = sem("v_staged")
        ring_filled = sem("ring_filled")
        ring_drained = sem("ring_drained")
        pv_done = sem("pv_done")
        acc_saved = sem("acc_saved")
        w_turned = sem("w_turned")
        w_scaled = sem("w_scaled")
        one_minus_set = sem("one_minus_set")
        tail_set = sem("tail_set")
        attn_turned = sem("attn_turned")
        sums_inverted = sem("sums_inverted")
        attn_scaled = sem("attn_scaled")
        x_added = sem("x_added")
        stats_taken = sem("stats_taken")
        h_stats = sem("h_stats")
        pool_small = sem("pool_small")
        h_rstd = sem("h_rstd")
        h_ready = sem("h_ready")
        h_turned = sem("h_turned")
        h_copied = sem("h_copied")
        k_ready = sem("k_ready")
        r_ready = sem("r_ready")
        relu_done = sem("relu_done")
        k_act_done = sem("k_act_done")
        gate_done = sem("gate_done")
        v_ready = sem("v_ready")
        gated = sem("gated")
        h_added = sem("h_added")
        z_stats = sem("z_stats")
        z_scale = sem("z_scale")
        o_ready = sem("o_ready")
        out_stored = sem("out_stored")

        x_tiles = x_in.rearrange("b (t p) c -> p (b t) c", p=P)
        out_tiles = out.rearrange("b (t p) c -> p (b t) c", p=P)
        x_chunks = x_sb[:, :, :].rearrange("p (n t) c -> p n t c", t=TC)

        block = ctx.enter_context(nc.Block())

        @block.sync
        def _(sp):
            for i in range(NC):
                sp.dma_start(x_sb[:, TC * i:TC * (i + 1), :], x_tiles[:, TC * i:TC * (i + 1), :]).then_inc(x_landed[i], 16)
                if i == 0:
                    for c, w in enumerate((rotation, entangle)):
                        sp.dma_start(columns[:, c:c + 1], w.rearrange("h (d o) -> (h d) o", o=1)).then_inc(columns_landed, 16)
                    for c, w in enumerate((mu_r, mu_k)):
                        sp.dma_start(columns[:, 2 + c:3 + c], w.rearrange("(c o) -> c o", o=1)).then_inc(columns_landed, 16)
            for i, w in enumerate((W_r, W_k, W_v)):
                sp.dma_start(w_sb[:, i, :], w).then_inc(w_landed, 16)

            def store_parts(b, g, which):
                dram = (q_parts_dram, k_parts_dram)[which]
                stored = parts_stored[2 if b else min(g, 1)]
                sp.dma_start(dram[b * GPB + g].rearrange("p c t -> c p t"),
                             qk_parts[g * GC:(g + 1) * GC, 2 * b + which, :, :]).then_inc(stored, 16)

            def load_stack(n, buf):
                for a in range(PARTS):
                    for b in range(PARTS):
                        r = (a * PARTS + b) * D
                        sp.dma_start(k_stack[r:r + D, buf], k_parts_dram[n, a].rearrange("(h d) t -> d h t", d=D))\
                            .then_inc(stack_landed[buf], 16)
                        for half in range(2):
                            sp.dma_start(q_stack[r:r + D, buf, half], q_parts_dram[n, b, :, half * HALF:(half + 1) * HALF]
                                         .rearrange("(h d) t -> d h t", d=D)).then_inc(stack_landed[buf], 16)

            def store_max_rows(half, buf):
                sp.dma_start(q_stack[TERMS:ROWS, buf, half].rearrange("p h t -> p (h t)"),
                             max_turned[:, half, :]).then_inc(max_row_landed[half], 16)

            for which in range(2):
                sp.wait_ge(dve_split, 3 * (which + 1))
                store_parts(0, 0, which)
            for which in range(2):
                for g in range(1, GPB):
                    store_parts(0, g, which)
            sp.wait_ge(ones_set, 1)
            sp.wait_ge(pool_ones_set, BUF - 1)
            sp.wait_ge(parts_stored[0], 2 * 16)
            load_stack(0, 0)
            sp.wait_ge(parts_stored[1], 2 * (GPB - 1) * 16)
            load_stack(1, 1)
            sp.wait_ge(ring_drained, 1)
            store_max_rows(0, 0)
            sp.wait_ge(pool_split, 6)
            for which in range(2):
                for g in range(GPB):
                    store_parts(1, g, which)
            sp.wait_ge(parts_stored[2], 2 * GPB * 16)

            def group(n, j, load=True, last=False):
                if load:
                    sp.wait_ge(ring_filled, 1 + FILLS * n)
                    load_stack(n + 2, (j + 2) % BUF)
                sp.wait_ge(ring_drained, turn_rank(n, 1) + 1)
                store_max_rows(1, j % BUF)
                if not last:
                    sp.wait_ge(ring_drained, turn_rank(n, 0) + 1)
                    store_max_rows(0, (j + 1) % BUF)

            with sp.Fori(0, (NG - 2) // BUF) as k:
                for j in range(BUF):
                    group(k * BUF + j, j)
            group(NG - 2, (NG - 2) % BUF, load=False)
            group(NG - 1, (NG - 1) % BUF, load=False, last=True)

            for c in range(NC):
                sp.wait_ge(o_ready, TC * (c + 1))
                sp.dma_start(out_tiles[:, TC * c:TC * (c + 1), :], o_sb[:, c, :, :]).then_inc(out_stored, 16)
            sp.wait_ge(out_stored, NC * 16)

        @block.tensor
        def _(pe):
            pe.wait_ge(ident_set, 2)
            for t in range(B * NT):
                if t % TC == 0:
                    pe.wait_ge(x_landed[t // TC], 16)
                tr = nc.tensor.transpose(ring_ps[:, t // TC, (t % TC) * P:(t % TC + 1) * P], x_sb[:, t, :], ident[:, :])
                if t % TC == TC - 1:
                    tr.then_inc(x_turned, 1)
            pe.wait_ge(w_landed, 3 * 16)
            for i in range(3):
                tr = nc.tensor.transpose(max_ps[:, 1, 1, i * P:(i + 1) * P], w_sb[:, i, :], ident[:, :])
            tr.then_inc(w_turned, 1)

            def max_unit(e, buf):
                tile, h = e // GH, e % GH
                for half in range(2):
                    mm = nc.tensor.matmul(max_ps[:, e % 2, half, :],
                                          q_stack[0:TERMS, buf, tile // HS2, h, tile % HS2 * P:(tile % HS2 + 1) * P],
                                          k_stack[0:TERMS, buf, h, half * HALF:(half + 1) * HALF],
                                          start=True, stop=True)
                mm.then_inc(rows_ready, 1)

            def turn_max(half, rank):
                nc.tensor.transpose(ring_ps[:, slot(rank), 0:P // 2].bitcast(BF16),
                                    max_parts[:, half, :, :].rearrange("p a r -> p (a r)"), ident_bf[:, :])\
                    .then_inc(ring_filled, 1)

            def score_tile(n, u, j, first, last):
                half, tile, h = u // (GH * HS), (u // GH) % NT, u % GH
                if not (first and u < RING - 1):
                    pe.wait_ge(ring_drained, fill_rank(n, u, last) - (RING - 1))
                nc.tensor.matmul(ring_ps[:, slot(fill_rank(0, u, last)), :],
                                 k_stack[:, j % BUF, h, tile * P:(tile + 1) * P],
                                 q_stack[:, j % BUF, half, h, :],
                                 start=True, stop=True).then_inc(ring_filled, 1)

            def weigh(n, s, j, last=False):
                tile = s % HS
                pe.wait_ge(ring_drained, fill_rank(n, GH * s + GH - 1, last) + 1)
                for h in range(GH):
                    mm = nc.tensor.matmul(ring_ps[VW * h:VW * (h + 1), RING, :],
                                          v_aug[:, j % BUF, tile, h, :], probs[:, s % 2, h, :],
                                          start=(tile == 0), stop=(tile == HS - 1), tile_position=(0, VW * h))
                mm.then_inc(pv_done, 1)

            def group(n, j, next_loads, first=False, last=False):
                for s in range(STEPS):
                    if s % HS == 0:
                        pe.wait_ge(max_row_landed[s // HS], 16 * (n + 1))
                    if s == TURN1 or (s == TURN0 and not last):
                        half = 1 if s == TURN1 else 0
                        pe.wait_ge(max_split, 8 * n + (8 if half else 12))
                        pe.wait_ge(ring_drained, turn_rank(n, half) - (RING - 1))
                        turn_max(half, turn_rank(0, half))
                    ahead = s + LEAD
                    for part in range(UNITS):
                        for u in range(GH * s + 2 * part, GH * s + 2 * (part + 1)):
                            score_tile(n, u, j, first, last)
                        if ahead < STEPS:
                            e = UNITS * ahead + part
                            pe.wait_ge(max_taken, GUNITS * n + e - 1)
                            max_unit(e, j % BUF)
                        elif not last:
                            e = UNITS * (ahead - STEPS) + part
                            if e == 0:
                                pe.wait_ge(stack_landed[(j + 1) % BUF], SLOADS * 16 * next_loads)
                            pe.wait_ge(max_taken, GUNITS * (n + 1) + e - 1)
                            max_unit(e, (j + 1) % BUF)
                    if s == 1:
                        pe.wait_ge(v_staged, n + 1)
                    if s % HS == 1 and not (first and s == 1):
                        pe.wait_ge(acc_saved, 2 * n + s // HS)
                    if s > 0:
                        weigh(n, s - 1, j, last)
                    elif not first:
                        weigh(n - 1, STEPS - 1, j - 1)

            pe.wait_ge(qk_scaled, 2 * 2 * B)
            pe.wait_ge(w_scaled, 5)
            pe.wait_ge(stack_landed[0], SLOADS * 16)
            for e in range(UNITS * LEAD):
                if e == UNITS * (LEAD - 1):
                    pe.wait_ge(max_split, 4)
                    turn_max(0, 0)
                if e >= 2:
                    pe.wait_ge(max_taken, e - 1)
                max_unit(e, 0)
            group(0, 0, 1, first=True)
            with pe.Fori(0, (NG - 2) // BUF) as k:
                for j in range(1, BUF + 1):
                    group(k * BUF + j, j, k + ((j + 1) // BUF + 1))
            group(NG - 1, (NG - 1) % BUF, 0, last=True)
            weigh(NG - 1, STEPS - 1, (NG - 1) % BUF, last=True)

            def turn_attention(c):
                if c == 0:
                    pe.wait_ge(acc_saved, 2 * NG)
                else:
                    pe.wait_ge(attn_scaled, c)
                b, first_token = c // 2, (c % 2) * BANK
                for t in range(TC):
                    for g in range(GPB):
                        tr = nc.tensor.transpose(
                            ring_ps[:, t, g * P:(g + 1) * P],
                            attn_T[:, b * GPB + g, first_token + t * P:first_token + (t + 1) * P], ident[:, :])
                tr.then_inc(attn_turned, 1)

            def turn_h(c):
                pe.wait_ge(h_ready, TC * (c + 1))
                if c == 0:
                    pe.wait_ge(max_taken, NG * GUNITS)
                else:
                    pe.wait_ge(h_copied, c)
                for t in range(TC):
                    tr = nc.tensor.transpose(max_ps[:, 0, 0, t * P:(t + 1) * P], h_sb[:, c, t, :], ident[:, :])
                tr.then_inc(h_turned, 1)

            def mix_in(c):
                b, at = c // 2, 1 + (c % 2) * BANK
                pe.wait_ge(h_copied, c + 1)
                if c == 0:
                    pe.wait_ge(tail_set, 2)
                else:
                    pe.wait_ge(relu_done, c)
                nc.tensor.matmul(max_ps[:, 0, 1, :], w_T[:, 2, :], h_T[:, b, at:at + BANK], start=True, stop=False)
                nc.tensor.matmul(max_ps[:, 0, 1, :], w_T[:, 3, :], h_T[:, b, at - 1:at - 1 + BANK],
                                 start=False, stop=True).then_inc(k_ready, 1)
                if c > 0:
                    pe.wait_ge(gate_done, c)
                for t in range(TC):
                    r = max_ps[:, 1, 0, t * C:(t + 1) * C]
                    nc.tensor.matmul(r, h_T[:, b, at + t * P:at + (t + 1) * P], w_T[:, 0, :], start=True, stop=False)
                    mm = nc.tensor.matmul(r, h_T[:, b, at - 1 + t * P:at - 1 + (t + 1) * P], w_T[:, 1, :],
                                          start=False, stop=True)
                mm.then_inc(r_ready, 1)

            def mix_out(c):
                pe.wait_ge(k_act_done, c + 1)
                if c > 0:
                    pe.wait_ge(gated, c)
                for t in range(TC):
                    mm = nc.tensor.matmul(max_ps[:, 1, 1, t * C:(t + 1) * C], k_act[:, c, t * P:(t + 1) * P],
                                          w_T[:, 4, :], start=True, stop=True)
                mm.then_inc(v_ready, 1)

            turn_attention(0)
            turn_attention(1)
            turn_h(0)
            mix_in(0)
            for c in range(1, NC):
                if c + 1 < NC:
                    turn_attention(c + 1)
                turn_h(c)
                mix_out(c - 1)
                mix_in(c)
            mix_out(NC - 1)

        @block.scalar
        def _(act):
            def scale_qk(b, which):
                x_T = ring_ps[:, 2 * b:2 * b + 2, :].rearrange("p k t -> p (k t)")
                nc.scalar.activation(qk_full[:, 2 * b + which, :], x_T, ACT.Identity,
                                     scale=columns[:, which:which + 1]).then_inc(qk_scaled, 1)
                nc.scalar.activation(qk_parts[:, 2 * b + which, 0, :], x_T, ACT.Identity,
                                     scale=columns[:, which:which + 1]).then_inc(qk_scaled, 1)

            act.wait_ge(columns_landed, 4 * 16)
            for b in range(B):
                act.wait_ge(x_turned, 2 * (b + 1))
                scale_qk(b, 0)
                scale_qk(b, 1)
            act.wait_ge(w_turned, 1)
            act.wait_ge(one_minus_set, 1)
            for i in range(2):
                turned = max_ps[:, 1, 1, i * P:(i + 1) * P]
                nc.scalar.activation(w_T[:, 2 * i, :], turned, ACT.Identity, scale=columns[:, 2 + i:3 + i]).then_inc(w_scaled, 1)
                nc.scalar.activation(w_T[:, 2 * i + 1, :], turned, ACT.Identity, scale=one_minus_mu[:, i:i + 1])\
                    .then_inc(w_scaled, 1)
            nc.scalar.activation(w_T[:, 4, :], max_ps[:, 1, 1, 2 * P:3 * P], ACT.Identity, scale=0.5).then_inc(w_scaled, 1)

            def copy_turned(half, rank):
                nc.scalar.activation(max_turned[:, half, :], ring_ps[0:MAXROWS, slot(rank), 0:P // 2].bitcast(BF16),
                                     ACT.Identity).then_inc(ring_drained, 1)

            def save_sums(n, half):
                act.wait_ge(pv_done, STEPS * n + HS * (half + 1))
                nc.scalar.activation(attn_T[:, n, half * HALF:(half + 1) * HALF], acc_ps, ACT.Identity).then_inc(acc_saved, 1)

            def group(n, first=False, last=False):
                for s in range(STEPS):
                    if s == TURN1 or (s == TURN0 and not last):
                        half = 1 if s == TURN1 else 0
                        act.wait_ge(ring_filled, turn_rank(n, half) + 1)
                        copy_turned(half, turn_rank(0, half))
                    if not (first and s < 2):
                        act.wait_ge(pv_done, STEPS * n + s - 1)
                    for h in range(GH):
                        u = GH * s + h
                        act.wait_ge(ring_filled, fill_rank(n, u, last) + 1)
                        nc.scalar.activation(probs[:, s % 2, h, :], ring_ps[:, slot(fill_rank(0, u, last)), :], ACT.Exp,
                                             scale=SCALE).then_inc(ring_drained, 1)
                    if s == 0 and not first:
                        save_sums(n - 1, 1)
                    if s == HS:
                        save_sums(n, 0)

            act.wait_ge(ring_filled, 1)
            copy_turned(0, 0)
            group(0, first=True)
            with act.Fori(0, (NG - 2) // BUF) as k:
                for j in range(1, BUF + 1):
                    group(k * BUF + j)
            group(NG - 1, last=True)
            save_sums(NG - 1, 1)

            def mix(c):
                b, at = c // 2, 1 + (c % 2) * BANK
                act.wait_ge(h_turned, c + 1)
                nc.scalar.activation(h_T[:, b, at:at + BANK], max_ps[:, 0, 0, :], ACT.Identity).then_inc(h_copied, 1)
                act.wait_ge(k_ready, c + 1)
                nc.scalar.activation(relu_k[:, c, :], max_ps[:, 0, 1, :], ACT.Relu).then_inc(relu_done, 1)
                act.wait_ge(relu_done, c + 1)
                nc.scalar.activation(k_act[:, c, :], relu_k[:, c, :], ACT.Square).then_inc(k_act_done, 1)
                act.wait_ge(r_ready, c + 1)
                nc.scalar.activation(gate[:, c, :, :].rearrange("p t c -> p (t c)"), max_ps[:, 1, 0, :], ACT.Tanh,
                                     scale=0.5).then_inc(gate_done, 1)

            def normalise_out(c):
                act.wait_ge(z_scale, c + 1)
                for t in range(TC):
                    nc.scalar.activation(o_sb[:, c, t, :], z_sb[:, c, t, :], ACT.Identity,
                                         scale=rstd[:, 1, c, t:t + 1], bias=neg_mean_rstd[:, c, t:t + 1]).then_inc(o_ready, 1)

            for c in range(NC):
                mix(c)
                if c >= 2:
                    normalise_out(c - 2)
            normalise_out(NC - 2)
            normalise_out(NC - 1)

        @block.vector
        def _(dve):
            nc.vector.memset(k_stack[2 * VW:ROWS, 0, :, :], 1.0).then_inc(ones_set, 1)
            dve.wait_ge(columns_landed, 4 * 16)
            nc.vector.tensor_scalar(one_minus_mu[:, :], columns[:, 2:4], -1.0, 1.0, ALU.mult, ALU.add).then_inc(one_minus_set, 1)
            for i in range(2):
                dve.wait_ge(qk_scaled, 2 * (i + 1))
                nc.vector.tensor_tensor(qk_rest[:, i, :], qk_full[:, i, :], qk_parts[:, i, 0, :], ALU.subtract)\
                    .then_inc(dve_split, 1)
                dve.wait_ge(dve_split, 3 * i + 1)
                nc.vector.tensor_copy(qk_parts[:, i, 1, :], qk_rest[:, i, :]).then_inc(dve_split, 1)
                dve.wait_ge(dve_split, 3 * i + 2)
                nc.vector.tensor_tensor(qk_parts[:, i, 2, :], qk_rest[:, i, :], qk_parts[:, i, 1, :], ALU.subtract)\
                    .then_inc(dve_split, 1)

            def take_max(n, e):
                tile, h = e // GH, e % GH
                column = h * (NT // 2) + tile % (NT // 2)
                dve.wait_ge(rows_ready, GUNITS * n + e + 1)
                nc.vector.tensor_reduce(neg_max[:, tile // (NT // 2), column:column + 1],
                                        max_ps[:, e % 2, :, :].rearrange("p k t -> p (k t)"), AX.X, ALU.max,
                                        negate=True).then_inc(max_taken, 1)

            with dve.Fori(0, NG) as n:
                for e in range(GUNITS):
                    take_max(n, e)

            def scale_attention(c):
                sums = ring_ps[:, :, :].rearrange("p t (h w) -> p (t h) w", w=VW)
                dve.wait_ge(attn_turned, c + 1)
                nc.vector.reciprocal(recip_sum[:, c, :], sums[:, :, D:D + 1].rearrange("p h o -> p (h o)")).then_inc(sums_inverted, 1)
                dve.wait_ge(sums_inverted, c + 1)
                nc.vector.tensor_tensor(y_sb[:, c, :, :].rearrange("p t (h d) -> p (t h) d", d=D), sums[:, :, 0:D],
                                        recip_sum[:, c, :].unsqueeze(2).to_broadcast([P, TC * H, D]), ALU.mult)\
                    .then_inc(attn_scaled, 1)

            def take_stats(norm, c, source, done, before):
                for t in range(TC):
                    nc.vector.bn_stats(stats[:, norm, c, t, :], source[:, c, t, :]).then_inc(stats_taken, 1)
                dve.wait_ge(stats_taken, TC * (before + 1))
                for t in range(TC):
                    nc.vector.bn_aggr(mean_var[:, norm, c, t, :], stats[:, norm, c, t, :]).then_inc(done, 1)

            def h_statistics(c, before):
                dve.wait_ge(x_added, c + 1)
                take_stats(0, c, y_sb, h_stats, before)

            def normalise_h(c):
                dve.wait_ge(h_rstd, c + 1)
                for t in range(TC):
                    nc.vector.tensor_scalar(h_sb[:, c, t, :], y_sb[:, c, t, :], mean_var[:, 0, c, t, 0:1],
                                            rstd[:, 0, c, t:t + 1], ALU.subtract, ALU.mult).then_inc(h_ready, 1)

            def apply_gate(c):
                dve.wait_ge(v_ready, c + 1)
                dve.wait_ge(gate_done, c + 1)
                nc.vector.scalar_tensor_tensor(out=z_sb[:, c, :, :].rearrange("p t c -> p (t c)"),
                                               in0=gate[:, c, :, :].rearrange("p t c -> p (t c)"), scalar=1.0,
                                               in1=max_ps[:, 1, 1, :], op0=ALU.add, op1=ALU.mult).then_inc(gated, 1)

            def z_statistics(c, before):
                dve.wait_ge(h_added, c + 1)
                take_stats(1, c, z_sb, z_stats, before)

            scale_attention(0)
            h_statistics(0, 0)
            scale_attention(1)
            normalise_h(0)
            h_statistics(1, 1)
            scale_attention(2)
            normalise_h(1)
            apply_gate(0)
            h_statistics(2, 2)
            scale_attention(3)
            z_statistics(0, 3)
            normalise_h(2)
            apply_gate(1)
            h_statistics(3, 4)
            z_statistics(1, 5)
            normalise_h(3)
            apply_gate(2)
            z_statistics(2, 6)
            apply_gate(3)
            z_statistics(3, 7)

        @block.gpsimd
        def _(pool):
            nc.gpsimd.memset(ident[:, :], 0.0).then_inc(ident_steps, 1)
            nc.gpsimd.memset(ident_bf[:, :], 0.0).then_inc(ident_steps, 1)
            pool.wait_ge(ident_steps, 2)
            for m in (ident, ident_bf):
                nc.gpsimd.affine_select(out=m[:, :], in_=m[:, :], compare_op=ALU.not_equal, fill=1.0, base=0,
                                        pattern=[[-1, P]], channel_multiplier=1).then_inc(ident_set, 1)
            pool.wait_ge(ident_set, 2)
            for buf in range(1, BUF):
                nc.gpsimd.memset(k_stack[2 * VW:ROWS, buf, :, :], 1.0).then_inc(pool_ones_set, 1)
            pool.wait_ge(pool_ones_set, BUF - 1)
            nc.gpsimd.memset(max_parts[:, :, :, :], 0.0).then_inc(v_cleared, 1)
            nc.gpsimd.memset(no_max[:, :], 0.0).then_inc(v_cleared, 1)
            nc.gpsimd.memset(v_aug[:, :, :, :, :], 0.0).then_inc(v_cleared, 1)
            pool.wait_ge(v_cleared, 3)
            nc.gpsimd.memset(v_aug[:, :, :, :, D:D + 1], 1.0).then_inc(v_cleared, 1)
            pool.wait_ge(v_cleared, 4)

            def stage_v(n, buf):
                src = x_sb[:, :, :].rearrange("p (b t) (g c) -> p b t g c", b=B, g=GPB)[:, n // GPB, :, n % GPB, :]
                nc.gpsimd.tensor_copy(v_aug[:, buf, :, :, 0:D], src.rearrange("p t (h d) -> p t h d", d=D)).then_inc(v_staged, 1)

            def split_max(n, half):
                done = 8 * n + 4 * half
                pool.wait_ge(max_taken, GUNITS * n + GUNITS // 2 * (half + 1))
                nc.gpsimd.tensor_tensor(max_parts[:, half, 0, :], neg_max[:, half, :], no_max[:, :], ALU.add).then_inc(max_split, 1)
                pool.wait_ge(max_split, done + 1)
                nc.gpsimd.tensor_tensor(max_rest[:, half, 0, :], neg_max[:, half, :], max_parts[:, half, 0, :], ALU.subtract)\
                    .then_inc(max_split, 1)
                pool.wait_ge(max_split, done + 2)
                nc.gpsimd.tensor_tensor(max_parts[:, half, 1, :], max_rest[:, half, 0, :], no_max[:, :], ALU.add).then_inc(max_split, 1)
                pool.wait_ge(max_split, done + 3)
                nc.gpsimd.tensor_tensor(max_parts[:, half, 2, :], max_rest[:, half, 0, :], max_parts[:, half, 1, :], ALU.subtract)\
                    .then_inc(max_split, 1)

            for i in range(NC):
                pool.wait_ge(x_landed[i], 16)
            stage_v(0, 0)
            for i in range(2):
                pool.wait_ge(qk_scaled, 2 * (2 + i + 1))
                nc.gpsimd.tensor_tensor(qk_rest[:, 2 + i, :], qk_full[:, 2 + i, :], qk_parts[:, 2 + i, 0, :], ALU.subtract)\
                    .then_inc(pool_split, 1)
                pool.wait_ge(pool_split, 3 * i + 1)
                nc.gpsimd.tensor_copy(qk_parts[:, 2 + i, 1, :], qk_rest[:, 2 + i, :]).then_inc(pool_split, 1)
                pool.wait_ge(pool_split, 3 * i + 2)
                nc.gpsimd.tensor_tensor(qk_parts[:, 2 + i, 2, :], qk_rest[:, 2 + i, :], qk_parts[:, 2 + i, 1, :], ALU.subtract)\
                    .then_inc(pool_split, 1)

            split_max(0, 0)

            def group(n, j):
                split_max(n, 1)
                stage_v(n + 1, (j + 1) % BUF)
                split_max(n + 1, 0)

            with pool.Fori(0, (NG - 2) // BUF) as k:
                for j in range(BUF):
                    group(k * BUF + j, j)
            group(NG - 2, (NG - 2) % BUF)
            split_max(NG - 1, 1)

            small = [0]

            def link(ins):
                small[0] += 1
                ins.then_inc(pool_small, 1)
                pool.wait_ge(pool_small, small[0])

            nc.gpsimd.memset(minus_half[:, :], -0.5).then_inc(tail_set, 1)
            nc.gpsimd.memset(h_T[:, :, 0:1], 0.0).then_inc(tail_set, 1)
            pool.wait_ge(tail_set, 2)

            def add_x(c):
                pool.wait_ge(attn_scaled, c + 1)
                nc.gpsimd.tensor_tensor(y_sb[:, c, :, :], y_sb[:, c, :, :], x_chunks[:, c, :, :], ALU.add).then_inc(x_added, 1)

            def h_scale(c):
                pool.wait_ge(h_stats, TC * (c + 1))
                link(nc.gpsimd.tensor_scalar(var_eps[:, 0, c, :], mean_var[:, 0, c, :, 1], EPS, None, ALU.add))
                nc.gpsimd.tensor_tensor(rstd[:, 0, c, :], var_eps[:, 0, c, :], minus_half[:, :], ALU.pow).then_inc(h_rstd, 1)

            def add_h(c):
                pool.wait_ge(gated, c + 1)
                nc.gpsimd.tensor_tensor(z_sb[:, c, :, :], z_sb[:, c, :, :], h_sb[:, c, :, :], ALU.add).then_inc(h_added, 1)

            def out_scale(c):
                pool.wait_ge(z_stats, TC * (c + 1))
                link(nc.gpsimd.tensor_scalar(var_eps[:, 1, c, :], mean_var[:, 1, c, :, 1], EPS, None, ALU.add))
                link(nc.gpsimd.tensor_tensor(rstd[:, 1, c, :], var_eps[:, 1, c, :], minus_half[:, :], ALU.pow))
                link(nc.gpsimd.tensor_tensor(mean_rstd[:, c, :], mean_var[:, 1, c, :, 0], rstd[:, 1, c, :], ALU.mult))
                nc.gpsimd.tensor_scalar(neg_mean_rstd[:, c, :], mean_rstd[:, c, :], -1.0, None, ALU.mult).then_inc(z_scale, 1)

            add_x(0)
            h_scale(0)
            add_x(1)
            h_scale(1)
            add_x(2)
            add_h(0)
            h_scale(2)
            add_x(3)
            out_scale(0)
            add_h(1)
            h_scale(3)
            out_scale(1)
            add_h(2)
            out_scale(2)
            add_h(3)
            out_scale(3)


_INS = ["L0_attn_inputs", "L0_attn_rotation_params", "L0_attn_entangle_params", "L0_ffn_W_r", "L0_ffn_W_k",
        "L0_ffn_W_v", "L0_ffn_mu_r", "L0_ffn_mu_k"]


def kernel(**inputs):
    import numpy as _np
    import concourse.bacc as _bacc
    from concourse import mybir as _mybir
    from concourse.bass_utils import run_bass_kernel_spmd as _run

    nc = _bacc.Bacc("TRN2", target_bir_lowering=False, num_devices=1)
    arrays, args = {}, []
    for name in _INS:
        a = _np.ascontiguousarray(inputs[name])
        arrays[f"in_{name}_dram"] = a
        args.append(nc.dram_tensor(f"in_{name}_dram", a.shape, _mybir.dt.from_np(a.dtype), kind="ExternalInput").ap())
    shape = inputs["L0_attn_inputs"].shape
    args.append(nc.dram_tensor("out_dram", shape, _mybir.dt.float32, kind="ExternalOutput").ap())
    build_attention_ffn(nc, *args)
    r = _run(nc, [arrays], core_ids=[0])
    return r.results[0]["out_dram"]
```

```python
from contextlib import ExitStack

import concourse.bass as bass
from concourse import mybir

ALU = mybir.AluOpType
ACT = mybir.ActivationFunctionType
F32 = mybir.dt.float32
BF16 = mybir.dt.bfloat16
AX = mybir.AxisListType


def build_attention_ffn(
    nc: bass.Bass,
    x_in: bass.AP,
    rotation: bass.AP,
    entangle: bass.AP,
    W_r: bass.AP,
    W_k: bass.AP,
    W_v: bass.AP,
    mu_r: bass.AP,
    mu_k: bass.AP,
    out: bass.AP,
):
    B, T, C = x_in.shape
    H, D = rotation.shape
    P = 128
    GH = 4
    GPB = H // GH
    NG = B * GPB
    GC = GH * D
    NT = T // P
    HS2 = NT // 2
    HALF = T // 2
    BANK = 512
    PARTS = 3
    TERMS = PARTS * PARTS * D
    MAX_ROW = P - PARTS
    VW = 32
    SCALE = float(D) ** -0.5
    EPS = 1e-5

    STEPS = 2 * NT
    HS = NT
    LEAD = HS + 3
    FREE = STEPS - LEAD
    UNITS = 2
    GUNITS = UNITS * STEPS
    TURN1 = HS - 2
    TURN0 = STEPS - 2
    RING = 3
    FILLS = GH * STEPS + 2
    BUF = 3
    SLOADS = 3 * PARTS
    MAXROWS = PARTS * 16
    PIECES = [(0, 4), (4, 4), (8, 4), (12, 2), (14, 2)]
    TC = BANK // C
    NC = B * NT // TC

    def fill_rank(n, unit, last=False):
        turned = (1 if unit >= GH * TURN1 else 0) + (1 if unit >= GH * TURN0 and not last else 0)
        return 1 + FILLS * n + unit + turned

    def turn_rank(n, which):
        return 1 + FILLS * n + (GH * TURN1 if which else GH * TURN0 + 1)

    def loads_counted(buf, loads):
        return 16 * (SLOADS * loads - (2 * PARTS if buf == 0 else 0))

    def slot(rank):
        return rank % RING

    with ExitStack() as ctx:
        def sb(name, shape, dt):
            return ctx.enter_context(nc.sbuf_tensor(name, shape, dt))

        def psum(name, shape, dt):
            return ctx.enter_context(nc.psum_tensor(name, shape, dt))

        def sem(name):
            return ctx.enter_context(nc.semaphore(name))

        q_parts_dram = nc.dram_tensor("q_parts", (B, PARTS, D, 2, H, HALF), BF16).ap()
        k_parts_dram = nc.dram_tensor("k_parts", (B, PARTS, D, H, T), BF16).ap()

        x_sb = sb("x_sb", [P, B * NT, C], F32)
        ident = sb("ident", [P, P], F32)
        ident_bf = sb("ident_bf", [P, P], BF16)
        columns = sb("columns", [P, 4], F32)
        qk_rest = sb("qk_rest", [P, 2 * B, T], F32)
        qk_parts = sb("qk_parts", [P, 2 * B, PARTS, T], BF16)
        q_stack = sb("q_stack", [P, BUF, 2, GH, HALF], BF16)
        k_stack = sb("k_stack", [P, BUF, GH, T], BF16)
        v_aug = sb("v_aug", [P, BUF, NT, GH, VW], F32)
        neg_max = sb("neg_max", [P, 2, 16], F32)
        max_rest = sb("max_rest", [P, 2, 2, 16], F32)
        max_parts = sb("max_parts", [P, 2, P // 16, 16], BF16)
        table_probe = sb("table_probe", [P, 1], F32)
        no_max = sb("no_max", [P, 16], F32)
        max_turned = sb("max_turned", [MAXROWS, 2, P], BF16)
        probs = sb("probs", [P, 2, GH, HALF], F32)
        attn_T = sb("attn_T", [P, NG, T], F32)

        recip_sum = sb("recip_sum", [P, B * NT, H], F32)
        y_sb = sb("y_sb", [P, B * NT, C], F32)
        h_sb = sb("h_sb", [P, B * NT, C], F32)
        stats = sb("stats", [P, 2, B * NT, 6], F32)
        mean_var = sb("mean_var", [P, 2, B * NT, 2], F32)
        var_eps = sb("var_eps", [P, 2, B * NT], F32)
        rstd = sb("rstd", [P, 2, B * NT], F32)
        minus_half = sb("minus_half", [P, TC], F32)
        neg_mean_rstd = sb("neg_mean_rstd", [P, B * NT], F32)
        w_sb = sb("w_sb", [P, 3, C], F32)
        w_T = sb("w_T", [P, 5, C], F32)
        one_minus_mu = sb("one_minus_mu", [P, 2], F32)
        h_T = sb("h_T", [P, B, 1 + T], F32)
        gate = sb("gate", [P, B * NT, C], F32)
        o_sb = sb("o_sb", [P, B * NT, C], F32)
        z_sb = qk_rest[:, 0:B, :].rearrange("p b (t c) -> p (b t) c", c=C)
        k_act = qk_rest[:, B:2 * B, :].rearrange("p b t -> p (b t)")

        ring_ps = psum("ring_ps", [P, RING + 1, BANK], F32)
        max_ps = psum("max_ps", [P, 2, 2, BANK], F32)

        acc_ps = ring_ps[:, RING, :]

        def turned_x(b):
            return ring_ps[:, 2 * b:2 * b + 2, :].rearrange("p k t -> p (k t)")

        x_landed = [sem(f"x_landed{i}") for i in range(4)]
        columns_landed = sem("columns_landed")
        w_landed = sem("w_landed")
        ident_steps = sem("ident_steps")
        ident_set = sem("ident_set")
        pool_rows_set = sem("pool_rows_set")
        ones_set = sem("ones_set")
        v_cleared = sem("v_cleared")
        table_loaded = sem("table_loaded")
        x_turned = sem("x_turned")
        x_turned_again = sem("x_turned_again")
        first_parts = sem("first_parts")
        rests_taken = sem("rests_taken")
        second_parts = sem("second_parts")
        third_parts = sem("third_parts")
        pool_third_parts = sem("pool_third_parts")
        early_stored = sem("early_stored")
        half_stored = [sem(f"half_stored{i}") for i in range(2)]
        first_half_landed = sem("first_half_landed")
        parts_stored = [sem(f"parts_stored{i}") for i in range(B)]
        stack_landed = [sem(f"stack_landed{i}") for i in range(BUF)]
        max_row_landed = [sem(f"max_row_landed{i}") for i in range(2)]
        rows_ready = sem("rows_ready")
        max_taken = sem("max_taken")
        max_split = sem("max_split")
        v_staged = sem("v_staged")
        ring_filled = sem("ring_filled")
        ring_drained = sem("ring_drained")
        pv_done = sem("pv_done")
        acc_saved = sem("acc_saved")
        w_turned = sem("w_turned")
        w_scaled = sem("w_scaled")
        one_minus_set = sem("one_minus_set")
        tail_set = sem("tail_set")
        attn_turned = sem("attn_turned")
        sums_inverted = sem("sums_inverted")
        attn_scaled = sem("attn_scaled")
        dve_linked = sem("dve_linked")
        x_added = sem("x_added")
        stats_taken = [sem(f"stats_taken{i}") for i in range(2)]
        averaged = [sem(f"averaged{i}") for i in range(2)]
        eps_added = [sem(f"eps_added{i}") for i in range(2)]
        rstd_ready = [sem(f"rstd_ready{i}") for i in range(2)]
        h_ready = sem("h_ready")
        h_turned = sem("h_turned")
        h_copied = sem("h_copied")
        k_ready = sem("k_ready")
        r_ready = sem("r_ready")
        k_act_done = sem("k_act_done")
        gate_done = sem("gate_done")
        v_ready = sem("v_ready")
        gated = sem("gated")
        z_scale = sem("z_scale")
        o_ready = sem("o_ready")
        dve_o_ready = sem("dve_o_ready")
        out_stored = sem("out_stored")

        def turn_banks(unit):
            return max_ps[:, 1 if unit in (1, B * NT // 2 - 1) else 0, :, :]

        def mix_bank(p, which):
            tokens = PIECES[p][1] * P
            return ring_ps[:, 2 * (p - 3) + which, 0:tokens] if p >= 3 else max_ps[:, 1, which, 0:tokens]

        def act_tiles(p):
            first, count = PIECES[p]
            return range(first, first + (count if count > 2 else 1))

        def tiles_of(p):
            return slice(PIECES[p][0], sum(PIECES[p]))

        x_tiles = x_in.rearrange("b (t p) c -> p (b t) c", p=P)
        out_tiles = out.rearrange("b (t p) c -> p (b t) c", p=P)

        block = ctx.enter_context(nc.Block())

        @block.sync
        def _(sp):
            for i in range(NC):
                sp.dma_start(x_sb[:, TC * i:TC * (i + 1), :], x_tiles[:, TC * i:TC * (i + 1), :]).then_inc(x_landed[i], 16)
                if i == NC // B - 1:
                    for c, w in enumerate((rotation, entangle)):
                        sp.dma_start(columns[:, c:c + 1], w.rearrange("h (d o) -> (h d) o", o=1)).then_inc(columns_landed, 16)
                    for c, w in enumerate((mu_r, mu_k)):
                        sp.dma_start(columns[:, 2 + c:3 + c], w.rearrange("(c o) -> c o", o=1)).then_inc(columns_landed, 16)
            for i, w in enumerate((W_r, W_k, W_v)):
                sp.dma_start(w_sb[:, i, :], w).then_inc(w_landed, 16)

            def store_part(b, which, part, stored, heads=(0, H), halves=(0, 1)):
                first, end = heads
                source = qk_parts[first * D:end * D, 2 * b + which, part, :]
                if which == 1:
                    sp.dma_start(k_parts_dram[b, part, :, first:end, :].rearrange("d h t -> h d t"), source).then_inc(stored, 16)
                else:
                    for half in halves:
                        sp.dma_start(q_parts_dram[b, part, :, half, first:end, :].rearrange("d h t -> h d t"),
                                     source[:, half * HALF:(half + 1) * HALF]).then_inc(stored, 16)

            def load_k_rows(n, buf, a, landed):
                source = k_parts_dram.rearrange("b a d (g h) t -> b g a d (h t)", h=GH)[n // GPB, n % GPB, a]
                sp.dma_start(k_stack[a * PARTS * D:(a + 1) * PARTS * D, buf].rearrange("r h t -> r (h t)"),
                             source.unsqueeze(1).to_broadcast([D, PARTS, GH * T])).then_inc(landed, 16)

            def load_q_rows(n, buf, a, half, landed):
                by_group = q_parts_dram.rearrange("b part d half (g h) t -> b g half d part (h t)", h=GH)
                sp.dma_start(q_stack[a * PARTS * D:(a + 1) * PARTS * D, buf, half].rearrange("r h t -> r (h t)"),
                             by_group[n // GPB, n % GPB, half]).then_inc(landed, 16)

            def load_stack(n, buf):
                for a in range(PARTS):
                    load_k_rows(n, buf, a, stack_landed[buf])
                    for half in range(2):
                        load_q_rows(n, buf, a, half, stack_landed[buf])

            def store_max_rows(half, buf):
                sp.dma_start(q_stack[MAX_ROW:P, buf, half].rearrange("p h t -> p (h t)"),
                             max_turned[:, half, :]).then_inc(max_row_landed[half], 16)

            for part, made in ((0, first_parts), (1, second_parts)):
                sp.wait_ge(made, 1)
                store_part(0, 0, part, half_stored[0], halves=(0,))
                store_part(0, 0, part, half_stored[1], halves=(1,))
                sp.wait_ge(made, 2)
                store_part(0, 1, part, early_stored)
            sp.wait_ge(third_parts, 1)
            store_part(0, 0, 2, half_stored[0], (0, GH), halves=(0,))
            sp.wait_ge(third_parts, 2)
            store_part(0, 1, 2, half_stored[0], (0, GH))
            sp.wait_ge(ones_set, 1)
            sp.wait_ge(pool_rows_set, 1)
            sp.wait_ge(early_stored, 2 * 16)
            for a in range(PARTS - 1):
                load_k_rows(0, 0, a, first_half_landed)
            store_part(0, 0, 2, half_stored[1], (0, GH), halves=(1,))
            sp.wait_ge(half_stored[0], 4 * 16)
            load_k_rows(0, 0, PARTS - 1, first_half_landed)
            for a in range(PARTS):
                load_q_rows(0, 0, a, 0, first_half_landed)
            sp.wait_ge(half_stored[1], 3 * 16)
            for a in range(PARTS):
                load_q_rows(0, 0, a, 1, stack_landed[0])
            for which in range(2):
                store_part(0, which, 2, parts_stored[0], (GH, H))
            sp.wait_ge(parts_stored[0], 3 * 16)
            sp.wait_ge(pool_rows_set, 2 * BUF - 1)
            load_stack(1, 1)
            for part, made in ((0, first_parts), (1, second_parts), (2, pool_third_parts)):
                for which in range(2):
                    sp.wait_ge(made, which + (1 if part == 2 else 3))
                    store_part(1, which, part, parts_stored[1])
            sp.wait_ge(ring_drained, 1)
            store_max_rows(0, 0)
            sp.wait_ge(parts_stored[1], 9 * 16)

            def group(n, j, load=True, last=False):
                if load:
                    sp.wait_ge(ring_filled, 1 + FILLS * n)
                    load_stack(n + 2, (j + 2) % BUF)
                sp.wait_ge(ring_drained, turn_rank(n, 1) + 1)
                store_max_rows(1, j % BUF)
                if not last:
                    sp.wait_ge(ring_drained, turn_rank(n, 0) + 1)
                    store_max_rows(0, (j + 1) % BUF)

            with sp.Fori(0, (NG - 2) // BUF) as k:
                for j in range(BUF):
                    group(k * BUF + j, j)
            group(NG - 2, (NG - 2) % BUF, load=False)
            group(NG - 1, (NG - 1) % BUF, load=False, last=True)

            for p in range(len(PIECES)):
                sp.wait_ge(o_ready, sum(len(act_tiles(i)) for i in range(p + 1)))
                if len(act_tiles(p)) < PIECES[p][1]:
                    sp.wait_ge(dve_o_ready, sum(PIECES[i][1] - len(act_tiles(i)) for i in range(p + 1)))
                sp.dma_start(out_tiles[:, tiles_of(p), :], o_sb[:, tiles_of(p), :]).then_inc(out_stored, 16)
            sp.wait_ge(out_stored, len(PIECES) * 16)

        @block.tensor
        def _(pe):
            pe.wait_ge(ident_set, 2)
            for t in range(B * NT):
                if t % TC == 0:
                    pe.wait_ge(x_landed[t // TC], 16)
                tr = nc.tensor.transpose(ring_ps[:, t // TC, (t % TC) * P:(t % TC + 1) * P], x_sb[:, t, :], ident[:, :])
                if t % TC == TC - 1:
                    tr.then_inc(x_turned, 1)
                if t == NT - 1:
                    for i in range(NT):
                        tr = nc.tensor.transpose(max_ps[:, 0, i // TC, (i % TC) * P:(i % TC + 1) * P], x_sb[:, i, :], ident[:, :])
                    tr.then_inc(x_turned_again, 1)
            pe.wait_ge(w_landed, 3 * 16)
            for i in range(3):
                tr = nc.tensor.transpose(max_ps[:, 1, 1, i * P:(i + 1) * P], w_sb[:, i, :], ident[:, :])
            tr.then_inc(w_turned, 1)

            def max_unit(e, buf):
                tile, h = e // GH, e % GH
                for half in range(2):
                    mm = nc.tensor.matmul(max_ps[:, e % 2, half, :],
                                          q_stack[0:MAX_ROW, buf, tile // HS2, h, tile % HS2 * P:(tile % HS2 + 1) * P],
                                          k_stack[0:MAX_ROW, buf, h, half * HALF:(half + 1) * HALF],
                                          start=True, stop=True)
                mm.then_inc(rows_ready, 1)

            def turn_max(half, rank):
                nc.tensor.transpose(ring_ps[:, slot(rank), 0:P // 2].bitcast(BF16),
                                    max_parts[:, half, :, :].rearrange("p a r -> p (a r)"), ident_bf[:, :])\
                    .then_inc(ring_filled, 1)

            def score_tile(n, u, j, first, last):
                half, tile, h = u // (GH * HS), (u // GH) % NT, u % GH
                if not (first and u < RING - 1):
                    pe.wait_ge(ring_drained, fill_rank(n, u, last) - (RING - 1))
                nc.tensor.matmul(ring_ps[:, slot(fill_rank(0, u, last)), :],
                                 k_stack[:, j % BUF, h, tile * P:(tile + 1) * P],
                                 q_stack[:, j % BUF, half, h, :],
                                 start=True, stop=True).then_inc(ring_filled, 1)

            def weigh(n, s, j, last=False):
                tile = s % HS
                pe.wait_ge(ring_drained, fill_rank(n, GH * s + GH - 1, last) + 1)
                for h in range(GH):
                    mm = nc.tensor.matmul(ring_ps[VW * h:VW * (h + 1), RING, :],
                                          v_aug[:, j % BUF, tile, h, :], probs[:, s % 2, h, :],
                                          start=(tile == 0), stop=(tile == HS - 1), tile_position=(0, VW * h))
                mm.then_inc(pv_done, 1)

            def turn_attention(tile, groups=range(GPB)):
                unit, b, half = tile // 2, tile // NT, tile % NT // HS2
                if tile == 0:
                    pe.wait_ge(max_taken, NG * GUNITS)
                elif tile % 2 == 0 and unit >= 2:
                    pe.wait_ge(attn_scaled, 1 if unit == 2 else min(unit, B * NT // 2 - 2))
                pe.wait_ge(acc_saved, 2 * (GPB * b + groups[-1]) + half + 1)
                token = tile % NT * P
                for g in groups:
                    tr = nc.tensor.transpose(turn_banks(unit)[:, tile % 2, g * P:(g + 1) * P],
                                             attn_T[:, b * GPB + g, token:token + P], ident[:, :])
                if groups[-1] == GPB - 1:
                    tr.then_inc(attn_turned, 1)

            def turn_h(p):
                pe.wait_ge(h_ready, sum(PIECES[p]))
                if 0 < p < 3:
                    pe.wait_ge(gate_done, p)
                for t in range(PIECES[p][1]):
                    tr = nc.tensor.transpose(mix_bank(p, 0)[:, t * P:(t + 1) * P], h_sb[:, PIECES[p][0] + t, :], ident[:, :])
                tr.then_inc(h_turned, 1)

            def h_at(p, back, tile=None):
                b, token = PIECES[p][0] // NT, PIECES[p][0] % NT * P
                first = 1 + token - back + (tile or 0) * P
                return h_T[:, b, first:first + (PIECES[p][1] * P if tile is None else P)]

            def mix_k(p, shift):
                if shift == 0:
                    pe.wait_ge(h_copied, p + 1)
                    if p == 0:
                        pe.wait_ge(tail_set, 2)
                    elif p < 3:
                        pe.wait_ge(gated, p)
                nc.tensor.matmul(mix_bank(p, 1), w_T[:, 2 + shift, :], h_at(p, shift),
                                 start=(shift == 0), stop=(shift == 1)).then_inc(k_ready, 1)

            def mix_r(p, t):
                pe.wait_ge(h_copied, p + 1)
                r = mix_bank(p, 0)[:, t * C:(t + 1) * C]
                nc.tensor.matmul(r, h_at(p, 0, t), w_T[:, 0, :], start=True, stop=False)
                nc.tensor.matmul(r, h_at(p, 1, t), w_T[:, 1, :], start=False, stop=True).then_inc(r_ready, 1)

            def mix_out(p, pair):
                pe.wait_ge(k_act_done, p + 1)
                for t in (2 * pair, 2 * pair + 1):
                    token = (PIECES[p][0] + t) * P
                    mm = nc.tensor.matmul(mix_bank(p, 1)[:, t * C:(t + 1) * C], k_act[:, token:token + P],
                                          w_T[:, 4, :], start=True, stop=True)
                mm.then_inc(v_ready, 1)

            def beside_last_group(place):
                if place in (1, 2, 3, 4, 5, 6):
                    turn_attention(place - 1)
                elif place in (12, 13):
                    turn_attention(6 + place - 12)
                elif place == 14:
                    turn_h(0)
                elif place in (16, 17):
                    mix_k(0, place - 16)
                elif 18 <= place < 22:
                    mix_r(0, place - 18)
                elif place in (22, 23):
                    mix_out(0, place - 22)
                elif place in (24, 25):
                    turn_attention(8 + place - 24)
                elif place == 26:
                    turn_h(1)
                elif place in (28, 29):
                    mix_k(1, place - 28)
                elif place in (30, 31):
                    turn_attention(10 + place - 30)
                elif 32 <= place < 36:
                    mix_r(1, place - 32)
                elif place in (36, 37):
                    mix_out(1, place - 36)
                elif place == 40:
                    turn_h(2)
                elif place in (43, 44):
                    mix_k(2, place - 43)
                elif 45 <= place < 49:
                    mix_r(2, place - 45)
                elif place in (49, 50):
                    mix_out(2, place - 49)
                elif place in (51, 52):
                    turn_attention(12 + place - 51, range(GPB - 1))
                elif place == 54:
                    pe.wait_ge(gate_done, 3)
                    pe.wait_ge(gated, 3)
                    turn_attention(14, range(GPB - 1))
                    turn_attention(15, range(GPB - 1))

            def group(n, j, next_loads, first=False, last=False):
                for s in range(STEPS):
                    if s % HS == 0:
                        pe.wait_ge(max_row_landed[s // HS], 16 * (n + 1))
                    if s == TURN1 or (s == TURN0 and not last):
                        half = 1 if s == TURN1 else 0
                        pe.wait_ge(max_split, 8 * n + (8 if half else 12))
                        pe.wait_ge(ring_drained, turn_rank(n, half) - (RING - 1))
                        turn_max(half, turn_rank(0, half))
                    ahead = s + LEAD
                    for part in range(UNITS):
                        for u in range(GH * s + 2 * part, GH * s + 2 * (part + 1)):
                            score_tile(n, u, j, first, last)
                            if last and s >= FREE:
                                beside_last_group((s - FREE) * (GH + 1) + u % GH)
                        if ahead < STEPS:
                            e = UNITS * ahead + part
                            pe.wait_ge(max_taken, GUNITS * n + e - 1)
                            max_unit(e, j % BUF)
                        elif not last:
                            e = UNITS * (ahead - STEPS) + part
                            if e == 0:
                                pe.wait_ge(stack_landed[(j + 1) % BUF], loads_counted((j + 1) % BUF, next_loads))
                            pe.wait_ge(max_taken, GUNITS * (n + 1) + e - 1)
                            max_unit(e, (j + 1) % BUF)
                    if s == 1:
                        pe.wait_ge(v_staged, n + 1)
                    if s % HS == 1 and not (first and s == 1):
                        pe.wait_ge(acc_saved, 2 * n + s // HS)
                    if s > 0:
                        weigh(n, s - 1, j, last)
                    elif not first:
                        weigh(n - 1, STEPS - 1, j - 1)
                    if last and s >= FREE:
                        beside_last_group((s - FREE) * (GH + 1) + GH)

            pe.wait_ge(first_parts, 2 * B)
            pe.wait_ge(rests_taken, 2 * B)
            pe.wait_ge(w_scaled, 5)
            pe.wait_ge(first_half_landed, 2 * PARTS * 16)
            for e in range(UNITS * LEAD):
                if e == UNITS * (LEAD - 1):
                    pe.wait_ge(max_split, 4)
                    turn_max(0, 0)
                if e >= 2:
                    pe.wait_ge(max_taken, e - 1)
                if e == GUNITS // 2:
                    pe.wait_ge(stack_landed[0], loads_counted(0, 1))
                max_unit(e, 0)
            group(0, 0, 1, first=True)
            with pe.Fori(0, (NG - 2) // BUF) as k:
                for j in range(1, BUF + 1):
                    group(k * BUF + j, j, k + ((j + 1) // BUF + 1))
            group(NG - 1, (NG - 1) % BUF, 0, last=True)
            weigh(NG - 1, STEPS - 1, (NG - 1) % BUF, last=True)

            for tile in range(PIECES[3][0], B * NT):
                turn_attention(tile, range(GPB - 1, GPB))
            turn_h(3)
            turn_h(4)
            mix_k(3, 0)
            mix_k(3, 1)
            mix_k(4, 0)
            mix_k(4, 1)
            for t in range(2):
                mix_r(3, t)
            mix_out(3, 0)
            for t in range(2):
                mix_r(4, t)
            mix_out(4, 0)

        @block.scalar
        def _(act):
            def first_part(b, which):
                nc.scalar.activation(qk_parts[:, 2 * b + which, 0, :], turned_x(b), ACT.Identity,
                                     scale=columns[:, which:which + 1]).then_inc(first_parts, 1)

            def second_part(b, which):
                act.wait_ge(rests_taken, 2 * b + which + 1)
                nc.scalar.activation(qk_parts[:, 2 * b + which, 1, :], qk_rest[:, 2 * b + which, :], ACT.Identity)\
                    .then_inc(second_parts, 1)

            act.wait_ge(ident_set, 2)
            nc.scalar.activation(table_probe[:, :], ident[:, 0:1], ACT.Exp).then_inc(table_loaded, 1)
            act.wait_ge(columns_landed, 4 * 16)
            for b in range(B):
                act.wait_ge(x_turned, 2 * (b + 1))
                first_part(b, 0)
                first_part(b, 1)
                second_part(b, 0)
                second_part(b, 1)
            act.wait_ge(w_turned, 1)
            act.wait_ge(one_minus_set, 1)
            for i in range(2):
                turned = max_ps[:, 1, 1, i * P:(i + 1) * P]
                nc.scalar.activation(w_T[:, 2 * i, :], turned, ACT.Identity, scale=columns[:, 2 + i:3 + i]).then_inc(w_scaled, 1)
                nc.scalar.activation(w_T[:, 2 * i + 1, :], turned, ACT.Identity, scale=one_minus_mu[:, i:i + 1])\
                    .then_inc(w_scaled, 1)
            nc.scalar.activation(w_T[:, 4, :], max_ps[:, 1, 1, 2 * P:3 * P], ACT.Identity, scale=0.5).then_inc(w_scaled, 1)

            def copy_turned(half, rank):
                nc.scalar.activation(max_turned[:, half, :], ring_ps[0:MAXROWS, slot(rank), 0:P // 2].bitcast(BF16),
                                     ACT.Identity).then_inc(ring_drained, 1)

            def save_sums(n, half):
                act.wait_ge(pv_done, STEPS * n + HS * (half + 1))
                nc.scalar.activation(attn_T[:, n, half * HALF:(half + 1) * HALF], acc_ps, ACT.Identity).then_inc(acc_saved, 1)

            def copy_h(p):
                b, token = PIECES[p][0] // NT, PIECES[p][0] % NT * P
                act.wait_ge(h_turned, p + 1)
                nc.scalar.activation(h_T[:, b, 1 + token:1 + token + PIECES[p][1] * P], mix_bank(p, 0), ACT.Identity)\
                    .then_inc(h_copied, 1)

            def take_gate(p):
                act.wait_ge(r_ready, sum(PIECES[p]))
                nc.scalar.activation(gate[:, tiles_of(p), :].rearrange("p t c -> p (t c)"), mix_bank(p, 0), ACT.Tanh,
                                     scale=0.5).then_inc(gate_done, 1)

            def normalise_out(p):
                act.wait_ge(z_scale, p + 1)
                for t in act_tiles(p):
                    nc.scalar.activation(o_sb[:, t, :], z_sb[:, t, :], ACT.Identity,
                                         scale=rstd[:, 1, t:t + 1], bias=neg_mean_rstd[:, t:t + 1]).then_inc(o_ready, 1)

            def before_exponential(place):
                if place == 15:
                    copy_h(0)
                elif place == 22:
                    take_gate(0)
                elif place == 27:
                    copy_h(1)
                elif place == 36:
                    take_gate(1)
                elif place == 41:
                    copy_h(2)
                elif place == 50:
                    take_gate(2)

            def group(n, first=False, last=False):
                for s in range(STEPS):
                    if s == TURN1 or (s == TURN0 and not last):
                        half = 1 if s == TURN1 else 0
                        act.wait_ge(ring_filled, turn_rank(n, half) + 1)
                        copy_turned(half, turn_rank(0, half))
                    if not (first and s < 2):
                        act.wait_ge(pv_done, STEPS * n + s - 1)
                    for h in range(GH):
                        u = GH * s + h
                        if last and s >= FREE:
                            before_exponential((s - FREE) * (GH + 1) + h)
                        act.wait_ge(ring_filled, fill_rank(n, u, last) + 1)
                        nc.scalar.activation(probs[:, s % 2, h, :], ring_ps[:, slot(fill_rank(0, u, last)), :], ACT.Exp,
                                             scale=SCALE).then_inc(ring_drained, 1)
                        if s == 1 and h == 0 and not first:
                            save_sums(n - 1, 1)
                        if s == HS + 1 and h == 0:
                            save_sums(n, 0)

            act.wait_ge(ring_filled, 1)
            copy_turned(0, 0)
            group(0, first=True)
            with act.Fori(0, (NG - 2) // BUF) as k:
                for j in range(1, BUF + 1):
                    group(k * BUF + j)
            group(NG - 1, last=True)
            save_sums(NG - 1, 1)

            for p in range(3):
                normalise_out(p)
            copy_h(3)
            copy_h(4)
            take_gate(3)
            take_gate(4)
            normalise_out(3)
            normalise_out(4)

        @block.vector
        def _(dve):
            nc.vector.memset(k_stack[P // 2:P, 0, :, :], 1.0).then_inc(ones_set, 1)
            dve.wait_ge(columns_landed, 4 * 16)
            nc.vector.tensor_scalar(one_minus_mu[:, :], columns[:, 2:4], -1.0, 1.0, ALU.mult, ALU.add).then_inc(one_minus_set, 1)
            def take_rest(b, which):
                dve.wait_ge(first_parts, which + 1 if b == 0 else 2 * B)
                x_T = max_ps[:, 0, :, :].rearrange("p k t -> p (k t)") if b == 0 else turned_x(b)
                nc.vector.scalar_tensor_tensor(out=qk_rest[:, 2 * b + which, :], in0=x_T, scalar=columns[:, which:which + 1],
                                               in1=qk_parts[:, 2 * b + which, 0, :], op0=ALU.mult, op1=ALU.subtract)\
                    .then_inc(rests_taken, 1)

            dve.wait_ge(x_turned_again, 1)
            for which in range(2):
                take_rest(0, which)
            for which in range(2):
                dve.wait_ge(second_parts, which + 1)
                dve.wait_ge(rests_taken, which + 1)
                nc.vector.tensor_tensor(qk_parts[:, which, 2, :], qk_rest[:, which, :], qk_parts[:, which, 1, :], ALU.subtract)\
                    .then_inc(third_parts, 1)
            for which in range(2):
                take_rest(1, which)

            def take_max(n, e):
                tile, h = e // GH, e % GH
                column = h * (NT // 2) + tile % (NT // 2)
                dve.wait_ge(rows_ready, GUNITS * n + e + 1)
                nc.vector.tensor_reduce(neg_max[:, tile // (NT // 2), column:column + 1],
                                        max_ps[:, e % 2, :, :].rearrange("p k t -> p (k t)"), AX.X, ALU.max,
                                        negate=True).then_inc(max_taken, 1)

            with dve.Fori(0, NG) as n:
                for e in range(GUNITS):
                    take_max(n, e)

            links = [0]

            def link(ins):
                links[0] += 1
                ins.then_inc(dve_linked, 1)
                dve.wait_ge(dve_linked, links[0])

            def scale_attention(unit):
                tiles = slice(2 * unit, 2 * unit + 2)
                heads = turn_banks(unit).rearrange("p t (h w) -> p t h w", w=VW)
                dve.wait_ge(attn_turned, 2 * (unit + 1))
                nc.vector.reciprocal(recip_sum[:, tiles, :], heads[:, :, :, D]).then_inc(sums_inverted, 1)
                dve.wait_ge(sums_inverted, unit + 1)
                nc.vector.tensor_tensor(y_sb[:, tiles, :].rearrange("p t (h d) -> p t h d", d=D), heads[:, :, :, 0:D],
                                        recip_sum[:, tiles, :].unsqueeze(3).to_broadcast([P, 2, H, D]), ALU.mult)\
                    .then_inc(attn_scaled, 1)

            def take_stats(norm, source, *pieces):
                for p in pieces:
                    for t in range(PIECES[p][0], sum(PIECES[p])):
                        nc.vector.bn_stats(stats[:, norm, t, :], source[:, t, :]).then_inc(stats_taken[norm], 1)
                for p in pieces:
                    dve.wait_ge(stats_taken[norm], sum(PIECES[p]))
                    for t in range(PIECES[p][0], sum(PIECES[p])):
                        nc.vector.bn_aggr(mean_var[:, norm, t, :], stats[:, norm, t, :]).then_inc(averaged[norm], 1)
                for p in pieces:
                    dve.wait_ge(averaged[norm], sum(PIECES[p]))
                    nc.vector.tensor_scalar(var_eps[:, norm, tiles_of(p)], mean_var[:, norm, tiles_of(p), 1], EPS, None, ALU.add)\
                        .then_inc(eps_added[norm], 1)

            def h_stats(*pieces):
                for p in pieces:
                    dve.wait_ge(attn_scaled, sum(PIECES[p]) // 2)
                    y = y_sb[:, tiles_of(p), :]
                    nc.vector.tensor_tensor(y, y, x_sb[:, tiles_of(p), :], ALU.add).then_inc(x_added, 1)
                dve.wait_ge(x_added, pieces[-1] + 1)
                take_stats(0, y_sb, *pieces)

            def norm_h(p):
                dve.wait_ge(rstd_ready[0], p + 1)
                for t in range(PIECES[p][0], sum(PIECES[p])):
                    nc.vector.tensor_scalar(h_sb[:, t, :], y_sb[:, t, :], mean_var[:, 0, t, 0:1],
                                            rstd[:, 0, t:t + 1], ALU.subtract, ALU.mult).then_inc(h_ready, 1)

            def square_k(p):
                first = PIECES[p][0] * P
                dve.wait_ge(k_ready, 2 * (p + 1))
                k = k_act[:, first:first + PIECES[p][1] * P]
                link(nc.vector.tensor_scalar(k, mix_bank(p, 1), 0.0, None, ALU.max))
                nc.vector.tensor_tensor(k, k, k, ALU.mult).then_inc(k_act_done, 1)

            def mix_h(p):
                z = z_sb[:, tiles_of(p), :]
                dve.wait_ge(v_ready, sum(PIECES[p]) // 2)
                dve.wait_ge(gate_done, p + 1)
                nc.vector.scalar_tensor_tensor(out=z.rearrange("p t c -> p (t c)"),
                                               in0=gate[:, tiles_of(p), :].rearrange("p t c -> p (t c)"), scalar=1.0,
                                               in1=mix_bank(p, 1), op0=ALU.add, op1=ALU.mult).then_inc(gated, 1)
                dve.wait_ge(gated, p + 1)
                dve.wait_ge(h_ready, sum(PIECES[p]))
                link(nc.vector.tensor_tensor(z, z, h_sb[:, tiles_of(p), :], ALU.add))
                take_stats(1, z_sb, p)

            def z_bias(p):
                dve.wait_ge(rstd_ready[1], p + 1)
                nc.vector.scalar_tensor_tensor(out=neg_mean_rstd[:, tiles_of(p)], in0=mean_var[:, 1, tiles_of(p), 0], scalar=-1.0,
                                               in1=rstd[:, 1, tiles_of(p)], op0=ALU.mult, op1=ALU.mult).then_inc(z_scale, 1)

            def normalise_out(p):
                t = PIECES[p][0] + 1
                nc.vector.tensor_scalar(o_sb[:, t, :], z_sb[:, t, :], mean_var[:, 1, t, 0:1],
                                        rstd[:, 1, t:t + 1], ALU.subtract, ALU.mult).then_inc(dve_o_ready, 1)

            scale_attention(0)
            scale_attention(1)
            h_stats(0)
            scale_attention(2)
            norm_h(0)
            scale_attention(3)
            h_stats(1)
            square_k(0)
            norm_h(1)
            scale_attention(4)
            mix_h(0)
            square_k(1)
            scale_attention(5)
            h_stats(2)
            z_bias(0)
            norm_h(2)
            mix_h(1)
            z_bias(1)
            square_k(2)
            mix_h(2)
            z_bias(2)
            scale_attention(6)
            scale_attention(7)
            h_stats(3, 4)
            norm_h(3)
            norm_h(4)
            square_k(3)
            square_k(4)
            mix_h(3)
            mix_h(4)
            z_bias(3)
            normalise_out(3)
            z_bias(4)
            normalise_out(4)

        @block.gpsimd
        def _(pool):
            nc.gpsimd.memset(ident[:, :], 0.0).then_inc(ident_steps, 1)
            nc.gpsimd.memset(ident_bf[:, :], 0.0).then_inc(ident_steps, 1)
            pool.wait_ge(ident_steps, 2)
            for m in (ident, ident_bf):
                nc.gpsimd.affine_select(out=m[:, :], in_=m[:, :], compare_op=ALU.not_equal, fill=1.0, base=0,
                                        pattern=[[-1, P]], channel_multiplier=1).then_inc(ident_set, 1)
            pool.wait_ge(ident_set, 2)
            for buf in range(BUF):
                nc.gpsimd.memset(q_stack[P // 2:P, buf].rearrange("p k h t -> p (k h t)").bitcast(F32), 0.0).then_inc(pool_rows_set, 1)
                if buf > 0:
                    nc.gpsimd.memset(k_stack[P // 2:P, buf, :, :], 1.0).then_inc(pool_rows_set, 1)
            pool.wait_ge(pool_rows_set, 2 * BUF - 1)
            nc.gpsimd.memset(max_parts[:, :, :, :], 0.0).then_inc(v_cleared, 1)
            nc.gpsimd.memset(no_max[:, :], 0.0).then_inc(v_cleared, 1)
            nc.gpsimd.memset(v_aug[:, :, :, :, :], 0.0).then_inc(v_cleared, 1)
            pool.wait_ge(v_cleared, 3)
            nc.gpsimd.memset(v_aug[:, :, :, :, D:D + 1], 1.0).then_inc(v_cleared, 1)
            pool.wait_ge(v_cleared, 4)

            def stage_v(n, buf):
                src = x_sb[:, :, :].rearrange("p (b t) (g c) -> p b t g c", b=B, g=GPB)[:, n // GPB, :, n % GPB, :]
                nc.gpsimd.tensor_copy(v_aug[:, buf, :, :, 0:D], src.rearrange("p t (h d) -> p t h d", d=D)).then_inc(v_staged, 1)

            def split_max(n, half):
                done = 8 * n + 4 * half
                pool.wait_ge(max_taken, GUNITS * n + GUNITS // 2 * (half + 1))
                nc.gpsimd.tensor_tensor(max_parts[:, half, 0, :], neg_max[:, half, :], no_max[:, :], ALU.add).then_inc(max_split, 1)
                pool.wait_ge(max_split, done + 1)
                nc.gpsimd.tensor_tensor(max_rest[:, half, 0, :], neg_max[:, half, :], max_parts[:, half, 0, :], ALU.subtract)\
                    .then_inc(max_split, 1)
                pool.wait_ge(max_split, done + 2)
                nc.gpsimd.tensor_tensor(max_parts[:, half, 1, :], max_rest[:, half, 0, :], no_max[:, :], ALU.add).then_inc(max_split, 1)
                pool.wait_ge(max_split, done + 3)
                nc.gpsimd.tensor_tensor(max_parts[:, half, 2, :], max_rest[:, half, 0, :], max_parts[:, half, 1, :], ALU.subtract)\
                    .then_inc(max_split, 1)

            for i in range(NC):
                pool.wait_ge(x_landed[i], 16)
            stage_v(0, 0)
            for which in range(2):
                pool.wait_ge(second_parts, 2 + which + 1)
                pool.wait_ge(rests_taken, 2 + which + 1)
                nc.gpsimd.tensor_tensor(qk_parts[:, 2 + which, 2, :], qk_rest[:, 2 + which, :], qk_parts[:, 2 + which, 1, :],
                                        ALU.subtract).then_inc(pool_third_parts, 1)

            split_max(0, 0)

            def group(n, j):
                split_max(n, 1)
                stage_v(n + 1, (j + 1) % BUF)
                split_max(n + 1, 0)

            with pool.Fori(0, (NG - 2) // BUF) as k:
                for j in range(BUF):
                    group(k * BUF + j, j)
            group(NG - 2, (NG - 2) % BUF)
            split_max(NG - 1, 1)

            nc.gpsimd.memset(h_T[:, :, 0:1], 0.0).then_inc(tail_set, 1)
            nc.gpsimd.memset(minus_half[:, :], -0.5).then_inc(tail_set, 1)
            pool.wait_ge(tail_set, 2)

            def take_rstd(norm, p):
                pool.wait_ge(eps_added[norm], p + 1)
                nc.gpsimd.tensor_tensor(rstd[:, norm, tiles_of(p)], var_eps[:, norm, tiles_of(p)],
                                        minus_half[:, 0:PIECES[p][1]], ALU.pow).then_inc(rstd_ready[norm], 1)

            take_rstd(0, 0)
            take_rstd(0, 1)
            take_rstd(1, 0)
            take_rstd(0, 2)
            take_rstd(1, 1)
            take_rstd(1, 2)
            take_rstd(0, 3)
            take_rstd(0, 4)
            take_rstd(1, 3)
            take_rstd(1, 4)


_INS = ["L0_attn_inputs", "L0_attn_rotation_params", "L0_attn_entangle_params", "L0_ffn_W_r", "L0_ffn_W_k",
        "L0_ffn_W_v", "L0_ffn_mu_r", "L0_ffn_mu_k"]


def kernel(**inputs):
    import numpy as _np
    import concourse.bacc as _bacc
    from concourse import mybir as _mybir
    from concourse.bass_utils import run_bass_kernel_spmd as _run

    nc = _bacc.Bacc("TRN2", target_bir_lowering=False, num_devices=1)
    arrays, args = {}, []
    for name in _INS:
        a = _np.ascontiguousarray(inputs[name])
        arrays[f"in_{name}_dram"] = a
        args.append(nc.dram_tensor(f"in_{name}_dram", a.shape, _mybir.dt.from_np(a.dtype), kind="ExternalInput").ap())
    shape = inputs["L0_attn_inputs"].shape
    args.append(nc.dram_tensor("out_dram", shape, _mybir.dt.float32, kind="ExternalOutput").ap())
    build_attention_ffn(nc, *args)
    r = _run(nc, [arrays], core_ids=[0])
    return r.results[0]["out_dram"]
```

```python
from contextlib import ExitStack

import concourse.bass as bass
from concourse import mybir

ALU = mybir.AluOpType
ACT = mybir.ActivationFunctionType
F32 = mybir.dt.float32
BF16 = mybir.dt.bfloat16
AX = mybir.AxisListType


def build_attention_ffn(
    nc: bass.Bass,
    x_in: bass.AP,
    rotation: bass.AP,
    entangle: bass.AP,
    W_r: bass.AP,
    W_k: bass.AP,
    W_v: bass.AP,
    mu_r: bass.AP,
    mu_k: bass.AP,
    out: bass.AP,
):
    B, T, C = x_in.shape
    H, D = rotation.shape
    P = 128
    GH = 4
    GPB = H // GH
    NG = B * GPB
    NT = T // P
    HS2 = NT // 2
    HALF = T // 2
    BANK = 512
    PARTS = 3
    MAX_ROW = P - PARTS
    VW = 32
    SCALE = float(D) ** -0.5
    EPS = 1e-5

    STEPS = 2 * NT
    HS = NT
    LEAD = HS + 3
    FREE = STEPS - LEAD
    UNITS = 2
    GUNITS = UNITS * STEPS
    TURN1 = HS - 2
    TURN0 = STEPS - 2
    RING = 3
    FILLS = GH * STEPS + 2
    BUF = 3
    SLOADS = 3 * PARTS
    MAXROWS = PARTS * 16
    PIECES = [(0, 4), (4, 4), (8, 4), (12, 2), (14, 2)]
    TC = BANK // C
    NC = B * NT // TC

    def fill_rank(n, unit, last=False):
        turned = (1 if unit >= GH * TURN1 else 0) + (1 if unit >= GH * TURN0 and not last else 0)
        return 1 + FILLS * n + unit + turned

    def turn_rank(n, which):
        return 1 + FILLS * n + (GH * TURN1 if which else GH * TURN0 + 1)

    def loads_counted(buf, loads):
        return 16 * (SLOADS * loads - (2 * PARTS if buf == 0 else 0))

    def slot(rank):
        return rank % RING

    with ExitStack() as ctx:
        def sb(name, shape, dt):
            return ctx.enter_context(nc.sbuf_tensor(name, shape, dt))

        def psum(name, shape, dt):
            return ctx.enter_context(nc.psum_tensor(name, shape, dt))

        def sem(name):
            return ctx.enter_context(nc.semaphore(name))

        q_parts_dram = nc.dram_tensor("q_parts", (B, PARTS, D, 2, H, HALF), BF16).ap()
        k_parts_dram = nc.dram_tensor("k_parts", (B, PARTS, D, H, T), BF16).ap()

        x_sb = sb("x_sb", [P, B * NT, C], F32)
        ident = sb("ident", [P, P], F32)
        ident_bf = sb("ident_bf", [P, P], BF16)
        columns = sb("columns", [P, 4], F32)
        qk_rest = sb("qk_rest", [P, 2 * B, T], F32)
        qk_parts = sb("qk_parts", [P, 2 * B, PARTS, T], BF16)
        q_stack = sb("q_stack", [P, BUF, 2, GH, HALF], BF16)
        k_stack = sb("k_stack", [P, BUF, GH, T], BF16)
        v_aug = sb("v_aug", [P, BUF, NT, GH, VW], F32)
        neg_max = sb("neg_max", [P, 2, 16], F32)
        max_rest = sb("max_rest", [P, 2, 2, 16], F32)
        max_parts = sb("max_parts", [P, 2, P // 16, 16], BF16)
        table_probe = sb("table_probe", [P, 1], F32)
        no_max = sb("no_max", [P, 16], F32)
        max_turned = sb("max_turned", [MAXROWS, 2, P], BF16)
        probs = sb("probs", [P, 2, GH, HALF], F32)
        attn_T = sb("attn_T", [P, NG, T], F32)

        recip_sum = sb("recip_sum", [P, B * NT, H], F32)
        y_sb = sb("y_sb", [P, B * NT, C], F32)
        h_sb = sb("h_sb", [P, B * NT, C], F32)
        stats = sb("stats", [P, 2, B * NT, 6], F32)
        mean_var = sb("mean_var", [P, 2, B * NT, 2], F32)
        var_eps = sb("var_eps", [P, 2, B * NT], F32)
        rstd = sb("rstd", [P, 2, B * NT], F32)
        minus_half = sb("minus_half", [P, TC], F32)
        neg_mean_rstd = sb("neg_mean_rstd", [P, B * NT], F32)
        w_sb = sb("w_sb", [P, 3, C], F32)
        w_T = sb("w_T", [P, 3, C], F32)
        h_T = sb("h_T", [P, B, 1 + T], F32)
        gate = sb("gate", [P, B * NT, C], F32)
        o_sb = sb("o_sb", [P, B * NT, C], F32)
        z_sb = qk_rest[:, 0:B, :].rearrange("p b (t c) -> p (b t) c", c=C)
        k_act = qk_rest[:, B:2 * B, :].rearrange("p b t -> p (b t)")

        parts_memory = qk_parts[:, :, :, :].rearrange("p i a t -> p (i a t)").bitcast(F32)
        change = parts_memory[:, 0:B * T]
        mixed = parts_memory[:, B * T:3 * B * T].rearrange("p (i t) -> p i t", i=2)

        ring_ps = psum("ring_ps", [P, RING + 1, BANK], F32)
        max_ps = psum("max_ps", [P, 2, 2, BANK], F32)

        acc_ps = ring_ps[:, RING, :]

        def turned_x(b):
            return ring_ps[:, 2 * b:2 * b + 2, :].rearrange("p k t -> p (k t)")

        FIRST_ORDER = [(1, 0), (0, 0), (1, 1), (0, 1)]
        ROW1 = len(FIRST_ORDER)

        x_landed = [sem(f"x_landed{i}") for i in range(4)]
        columns_landed = [sem(f"columns_landed{i}") for i in range(2)]
        w_landed = sem("w_landed")
        ident_steps = sem("ident_steps")
        ident_set = sem("ident_set")
        pool_rows_set = sem("pool_rows_set")
        ones_set = sem("ones_set")
        v_cleared = sem("v_cleared")
        table_loaded = sem("table_loaded")
        x_turned = sem("x_turned")
        first_parts = sem("first_parts")
        rests_taken = sem("rests_taken")
        second_parts = sem("second_parts")
        third_parts = sem("third_parts")
        pool_third_parts = sem("pool_third_parts")
        k_stored = [sem(f"k_stored{i}") for i in range(PARTS)]
        half_stored = [sem(f"half_stored{i}") for i in range(2)]
        first_half_landed = sem("first_half_landed")
        parts_stored = [sem(f"parts_stored{i}") for i in range(B)]
        stack_landed = [sem(f"stack_landed{i}") for i in range(BUF)]
        max_row_landed = [sem(f"max_row_landed{i}") for i in range(2)]
        rows_ready = sem("rows_ready")
        max_taken = sem("max_taken")
        max_split = sem("max_split")
        v_staged = sem("v_staged")
        ring_filled = sem("ring_filled")
        ring_drained = sem("ring_drained")
        pv_done = sem("pv_done")
        acc_saved = sem("acc_saved")
        w_turned = sem("w_turned")
        w_scaled = sem("w_scaled")
        tail_set = sem("tail_set")
        attn_turned = sem("attn_turned")
        early_turned = sem("early_turned")
        early_scaled = sem("early_scaled")
        sums_inverted = sem("sums_inverted")
        attn_scaled = sem("attn_scaled")
        dve_linked = sem("dve_linked")
        x_added = sem("x_added")
        stats_taken = [sem(f"stats_taken{i}") for i in range(2)]
        averaged = [sem(f"averaged{i}") for i in range(2)]
        eps_added = [sem(f"eps_added{i}") for i in range(2)]
        rstd_ready = [sem(f"rstd_ready{i}") for i in range(2)]
        h_ready = sem("h_ready")
        h_turned = sem("h_turned")
        h_copied = sem("h_copied")
        k_mixed = sem("k_mixed")
        r_mixed = sem("r_mixed")
        k_ready = sem("k_ready")
        r_ready = sem("r_ready")
        k_act_done = sem("k_act_done")
        gate_done = sem("gate_done")
        v_ready = sem("v_ready")
        gated = sem("gated")
        h_added = sem("h_added")
        z_scale = sem("z_scale")
        o_ready = sem("o_ready")
        dve_o_ready = sem("dve_o_ready")
        out_stored = sem("out_stored")

        OTHER_BANKS = (1, 3, B * NT // 2 - 1)

        def turn_banks(unit):
            return max_ps[:, 1 if unit in OTHER_BANKS else 0, :, :]

        def mix_bank(p, which):
            tokens = PIECES[p][1] * P
            return ring_ps[:, 2 * (p - 3) + which, 0:tokens] if p >= 3 else max_ps[:, 1, which, 0:tokens]

        def act_tiles(p):
            first, count = PIECES[p]
            return range(first, first + (count if count > 2 else 1))

        def tiles_of(p):
            return slice(PIECES[p][0], sum(PIECES[p]))

        x_tiles = x_in.rearrange("b (t p) c -> p (b t) c", p=P)
        out_tiles = out.rearrange("b (t p) c -> p (b t) c", p=P)

        block = ctx.enter_context(nc.Block())

        @block.sync
        def _(sp):
            for i in range(NC):
                sp.dma_start(x_sb[:, TC * i:TC * (i + 1), :], x_tiles[:, TC * i:TC * (i + 1), :]).then_inc(x_landed[i], 16)
                if i == NC // B - 1:
                    for c, w in enumerate((rotation, entangle)):
                        sp.dma_start(columns[:, c:c + 1], w.rearrange("h (d o) -> (h d) o", o=1)).then_inc(columns_landed[0], 16)
            for c, w in enumerate((mu_r, mu_k)):
                sp.dma_start(columns[:, 2 + c:3 + c], w.rearrange("(c o) -> c o", o=1)).then_inc(columns_landed[1], 16)
            for i, w in enumerate((W_r, W_k, W_v)):
                sp.dma_start(w_sb[:, i, :], w).then_inc(w_landed, 16)

            def store_part(b, which, part, stored, heads=(0, H), halves=(0, 1)):
                first, end = heads
                source = qk_parts[first * D:end * D, 2 * b + which, part, :]
                if which == 1:
                    sp.dma_start(k_parts_dram[b, part, :, first:end, :].rearrange("d h t -> h d t"), source).then_inc(stored, 16)
                else:
                    for half in halves:
                        sp.dma_start(q_parts_dram[b, part, :, half, first:end, :].rearrange("d h t -> h d t"),
                                     source[:, half * HALF:(half + 1) * HALF]).then_inc(stored, 16)

            def load_k_rows(n, buf, a, landed):
                source = k_parts_dram.rearrange("b a d (g h) t -> b g a d (h t)", h=GH)[n // GPB, n % GPB, a]
                sp.dma_start(k_stack[a * PARTS * D:(a + 1) * PARTS * D, buf].rearrange("r h t -> r (h t)"),
                             source.unsqueeze(1).to_broadcast([D, PARTS, GH * T])).then_inc(landed, 16)

            def load_q_rows(n, buf, a, half, landed):
                by_group = q_parts_dram.rearrange("b part d half (g h) t -> b g half d part (h t)", h=GH)
                sp.dma_start(q_stack[a * PARTS * D:(a + 1) * PARTS * D, buf, half].rearrange("r h t -> r (h t)"),
                             by_group[n // GPB, n % GPB, half]).then_inc(landed, 16)

            def load_stack(n, buf):
                for a in range(PARTS):
                    load_k_rows(n, buf, a, stack_landed[buf])
                    for half in range(2):
                        load_q_rows(n, buf, a, half, stack_landed[buf])

            def store_max_rows(half, buf):
                sp.dma_start(q_stack[MAX_ROW:P, buf, half].rearrange("p h t -> p (h t)"),
                             max_turned[:, half, :]).then_inc(max_row_landed[half], 16)

            sp.wait_ge(first_parts, 2)
            store_part(0, 0, 0, half_stored[0], halves=(0,))
            sp.wait_ge(first_parts, 3)
            store_part(0, 1, 0, k_stored[0])
            sp.wait_ge(second_parts, 2)
            store_part(0, 0, 1, half_stored[0], halves=(0,))
            sp.wait_ge(second_parts, 3)
            store_part(0, 1, 1, k_stored[1])
            sp.wait_ge(third_parts, 2)
            store_part(0, 0, 2, half_stored[0], (0, GH), halves=(0,))
            sp.wait_ge(third_parts, 3)
            store_part(0, 1, 2, k_stored[2], (0, GH))
            sp.wait_ge(ones_set, 1)
            sp.wait_ge(pool_rows_set, 1)
            for a in range(PARTS):
                sp.wait_ge(k_stored[a], 16)
                load_k_rows(0, 0, a, first_half_landed)
                if a == 1:
                    sp.wait_ge(half_stored[0], PARTS * 16)
                    load_q_rows(0, 0, 0, 0, first_half_landed)
            for a in range(1, PARTS):
                load_q_rows(0, 0, a, 0, first_half_landed)
            sp.wait_ge(first_parts, 4)
            store_part(0, 0, 0, half_stored[1], halves=(1,))
            sp.wait_ge(second_parts, 4)
            store_part(0, 0, 1, half_stored[1], halves=(1,))
            sp.wait_ge(third_parts, 4)
            store_part(0, 0, 2, half_stored[1], (0, GH), halves=(1,))
            sp.wait_ge(half_stored[1], 3 * 16)
            for a in range(PARTS):
                load_q_rows(0, 0, a, 1, stack_landed[0])
            for which in range(2):
                store_part(0, which, 2, parts_stored[0], (GH, H))
            sp.wait_ge(parts_stored[0], 3 * 16)
            sp.wait_ge(pool_rows_set, 2 * BUF - 1)
            load_stack(1, 1)
            for part, made, before in ((0, first_parts, ROW1), (1, second_parts, ROW1), (2, pool_third_parts, 0)):
                for which in (1, 0):
                    sp.wait_ge(made, before + 2 - which)
                    store_part(1, which, part, parts_stored[1])
            sp.wait_ge(ring_drained, 1)
            store_max_rows(0, 0)
            sp.wait_ge(parts_stored[1], 9 * 16)

            def group(n, j, load=True, last=False):
                if load:
                    sp.wait_ge(ring_filled, 1 + FILLS * n)
                    load_stack(n + 2, (j + 2) % BUF)
                sp.wait_ge(ring_drained, turn_rank(n, 1) + 1)
                store_max_rows(1, j % BUF)
                if not last:
                    sp.wait_ge(ring_drained, turn_rank(n, 0) + 1)
                    store_max_rows(0, (j + 1) % BUF)

            with sp.Fori(0, (NG - 2) // BUF) as k:
                for j in range(BUF):
                    group(k * BUF + j, j)
            group(NG - 2, (NG - 2) % BUF, load=False)
            group(NG - 1, (NG - 1) % BUF, load=False, last=True)

            for p in range(len(PIECES)):
                sp.wait_ge(o_ready, sum(len(act_tiles(i)) for i in range(p + 1)))
                if len(act_tiles(p)) < PIECES[p][1]:
                    sp.wait_ge(dve_o_ready, sum(PIECES[i][1] - len(act_tiles(i)) for i in range(p + 1)))
                sp.dma_start(out_tiles[:, tiles_of(p), :], o_sb[:, tiles_of(p), :]).then_inc(out_stored, 16)
            sp.wait_ge(out_stored, len(PIECES) * 16)

        @block.tensor
        def _(pe):
            pe.wait_ge(ident_set, 2)
            for t in range(B * NT):
                if t % TC == 0:
                    pe.wait_ge(x_landed[t // TC], 16)
                tr = nc.tensor.transpose(ring_ps[:, t // TC, (t % TC) * P:(t % TC + 1) * P], x_sb[:, t, :], ident[:, :])
                if t % TC == TC - 1:
                    tr.then_inc(x_turned, 1)
            pe.wait_ge(w_landed, 3 * 16)
            for i in range(3):
                tr = nc.tensor.transpose(max_ps[:, 1, 1, i * P:(i + 1) * P], w_sb[:, i, :], ident[:, :])
            tr.then_inc(w_turned, 1)

            def max_unit(e, buf):
                tile, h = e // GH, e % GH
                for half in range(2):
                    mm = nc.tensor.matmul(max_ps[:, e % 2, half, :],
                                          q_stack[0:MAX_ROW, buf, tile // HS2, h, tile % HS2 * P:(tile % HS2 + 1) * P],
                                          k_stack[0:MAX_ROW, buf, h, half * HALF:(half + 1) * HALF],
                                          start=True, stop=True)
                mm.then_inc(rows_ready, 1)

            def turn_max(half, rank):
                nc.tensor.transpose(ring_ps[:, slot(rank), 0:P // 2].bitcast(BF16),
                                    max_parts[:, half, :, :].rearrange("p a r -> p (a r)"), ident_bf[:, :])\
                    .then_inc(ring_filled, 1)

            def score_tile(n, u, j, first, last):
                half, tile, h = u // (GH * HS), (u // GH) % NT, u % GH
                if not (first and u < RING - 1):
                    pe.wait_ge(ring_drained, fill_rank(n, u, last) - (RING - 1))
                nc.tensor.matmul(ring_ps[:, slot(fill_rank(0, u, last)), :],
                                 k_stack[:, j % BUF, h, tile * P:(tile + 1) * P],
                                 q_stack[:, j % BUF, half, h, :],
                                 start=True, stop=True).then_inc(ring_filled, 1)

            def weigh(n, s, j, last=False):
                tile = s % HS
                pe.wait_ge(ring_drained, fill_rank(n, GH * s + GH - 1, last) + 1)
                for h in range(GH):
                    mm = nc.tensor.matmul(ring_ps[VW * h:VW * (h + 1), RING, :],
                                          v_aug[:, j % BUF, tile, h, :], probs[:, s % 2, h, :],
                                          start=(tile == 0), stop=(tile == HS - 1), tile_position=(0, VW * h))
                mm.then_inc(pv_done, 1)

            def turn_attention(tile, groups=range(GPB)):
                unit, b, half = tile // 2, tile // NT, tile % NT // HS2
                if tile == 0:
                    pe.wait_ge(max_taken, NG * GUNITS)
                elif tile % 2 == 0 and unit >= 2:
                    before = [u for u in range(unit) if (u in OTHER_BANKS) == (unit in OTHER_BANKS)][-1]
                    pe.wait_ge(attn_scaled, before + 1)
                pe.wait_ge(acc_saved, 2 * (GPB * b + groups[-1]) + half + 1)
                token = tile % NT * P
                for g in groups:
                    tr = nc.tensor.transpose(turn_banks(unit)[:, tile % 2, g * P:(g + 1) * P],
                                             attn_T[:, b * GPB + g, token:token + P], ident[:, :])
                tr.then_inc(attn_turned if groups[-1] == GPB - 1 else early_turned, 1)

            def turn_h(p):
                pe.wait_ge(h_ready, sum(PIECES[p]))
                if p == 0:
                    pe.wait_ge(attn_scaled, 4)
                if 0 < p < 3:
                    pe.wait_ge(gate_done, p)
                for t in range(PIECES[p][1]):
                    tr = nc.tensor.transpose(mix_bank(p, 0)[:, t * P:(t + 1) * P], h_sb[:, PIECES[p][0] + t, :], ident[:, :])
                tr.then_inc(h_turned, 1)

            def mix_k(p):
                pe.wait_ge(k_mixed, p + 1)
                if 0 < p < 3:
                    pe.wait_ge(gated, p)
                first = PIECES[p][0] * P
                nc.tensor.matmul(mix_bank(p, 1), w_T[:, 1, :], mixed[:, 1, first:first + PIECES[p][1] * P],
                                 start=True, stop=True).then_inc(k_ready, 1)

            def mix_r(p, pair):
                pe.wait_ge(r_mixed, p + 1)
                for t in (2 * pair, 2 * pair + 1):
                    token = (PIECES[p][0] + t) * P
                    mm = nc.tensor.matmul(mix_bank(p, 0)[:, t * C:(t + 1) * C], mixed[:, 0, token:token + P], w_T[:, 0, :],
                                          start=True, stop=True)
                mm.then_inc(r_ready, 1)

            def mix_out(p, pair):
                pe.wait_ge(k_act_done, p + 1)
                for t in (2 * pair, 2 * pair + 1):
                    token = (PIECES[p][0] + t) * P
                    mm = nc.tensor.matmul(mix_bank(p, 1)[:, t * C:(t + 1) * C], k_act[:, token:token + P],
                                          w_T[:, 2, :], start=True, stop=True)
                mm.then_inc(v_ready, 1)

            def beside_last_group(place):
                if 1 <= place < 9:
                    turn_attention(place - 1)
                elif place == 12:
                    turn_h(0)
                elif place == 16:
                    mix_k(0)
                elif place in (17, 18):
                    mix_r(0, place - 17)
                elif place in (20, 21):
                    mix_out(0, place - 20)
                elif place in (22, 23):
                    turn_attention(8 + place - 22)
                elif place == 24:
                    turn_h(1)
                elif place in (25, 26):
                    turn_attention(10 + place - 25)
                elif place == 29:
                    mix_k(1)
                elif place in (30, 31):
                    mix_r(1, place - 30)
                elif place in (34, 35):
                    mix_out(1, place - 34)
                elif place == 37:
                    turn_h(2)
                elif place == 41:
                    mix_k(2)
                elif place in (42, 43):
                    mix_r(2, place - 42)
                elif place in (46, 47):
                    mix_out(2, place - 46)
                elif place in (51, 52):
                    turn_attention(12 + place - 51, range(GPB - 1))
                elif place == 54:
                    pe.wait_ge(gate_done, 3)
                    pe.wait_ge(gated, 3)
                    turn_attention(14, range(GPB - 1))
                    turn_attention(15, range(GPB - 1))

            def group(n, j, next_loads, first=False, last=False):
                for s in range(STEPS):
                    if s % HS == 0:
                        pe.wait_ge(max_row_landed[s // HS], 16 * (n + 1))
                    if s == TURN1 or (s == TURN0 and not last):
                        half = 1 if s == TURN1 else 0
                        pe.wait_ge(max_split, 8 * n + (8 if half else 12))
                        pe.wait_ge(ring_drained, turn_rank(n, half) - (RING - 1))
                        turn_max(half, turn_rank(0, half))
                    ahead = s + LEAD
                    for part in range(UNITS):
                        for u in range(GH * s + 2 * part, GH * s + 2 * (part + 1)):
                            score_tile(n, u, j, first, last)
                            if last and s >= FREE:
                                beside_last_group((s - FREE) * (GH + 1) + u % GH)
                        if ahead < STEPS:
                            e = UNITS * ahead + part
                            pe.wait_ge(max_taken, GUNITS * n + e - 1)
                            max_unit(e, j % BUF)
                        elif not last:
                            e = UNITS * (ahead - STEPS) + part
                            if e == 0:
                                pe.wait_ge(stack_landed[(j + 1) % BUF], loads_counted((j + 1) % BUF, next_loads))
                            pe.wait_ge(max_taken, GUNITS * (n + 1) + e - 1)
                            max_unit(e, (j + 1) % BUF)
                    if s == 1:
                        pe.wait_ge(v_staged, n + 1)
                    if s % HS == 1 and not (first and s == 1):
                        pe.wait_ge(acc_saved, 2 * n + s // HS)
                    if s > 0:
                        weigh(n, s - 1, j, last)
                    elif not first:
                        weigh(n - 1, STEPS - 1, j - 1)
                    if last and s >= FREE:
                        beside_last_group((s - FREE) * (GH + 1) + GH)

            pe.wait_ge(first_parts, ROW1 + 2)
            pe.wait_ge(rests_taken, ROW1 + 2)
            pe.wait_ge(w_scaled, 2)
            pe.wait_ge(first_half_landed, 2 * PARTS * 16)
            for e in range(UNITS * LEAD):
                if e == UNITS * (LEAD - 1):
                    pe.wait_ge(max_split, 4)
                    turn_max(0, 0)
                if e >= 2:
                    pe.wait_ge(max_taken, e - 1)
                if e == GUNITS // 2:
                    pe.wait_ge(stack_landed[0], loads_counted(0, 1))
                max_unit(e, 0)
            group(0, 0, 1, first=True)
            with pe.Fori(0, (NG - 2) // BUF) as k:
                for j in range(1, BUF + 1):
                    group(k * BUF + j, j, k + ((j + 1) // BUF + 1))
            group(NG - 1, (NG - 1) % BUF, 0, last=True)
            weigh(NG - 1, STEPS - 1, (NG - 1) % BUF, last=True)

            pe.wait_ge(early_scaled, 1)
            for tile in range(PIECES[3][0], B * NT):
                turn_attention(tile, range(GPB - 1, GPB))
            turn_h(3)
            turn_h(4)
            mix_k(3)
            mix_k(4)
            mix_r(3, 0)
            mix_out(3, 0)
            mix_r(4, 0)
            mix_out(4, 0)

        @block.scalar
        def _(act):
            def first_part(b, which, tokens=slice(0, T)):
                nc.scalar.activation(qk_parts[:, 2 * b + which, 0, tokens], turned_x(b)[:, tokens], ACT.Identity,
                                     scale=columns[:, which:which + 1]).then_inc(first_parts, 1)

            def second_part(b, which, rank, tokens=slice(0, T)):
                act.wait_ge(rests_taken, rank)
                nc.scalar.activation(qk_parts[:, 2 * b + which, 1, tokens], qk_rest[:, 2 * b + which, tokens], ACT.Identity)\
                    .then_inc(second_parts, 1)

            def half_of(half):
                return slice(half * HALF, (half + 1) * HALF)

            act.wait_ge(ident_set, 2)
            nc.scalar.activation(table_probe[:, :], ident[:, 0:1], ACT.Exp).then_inc(table_loaded, 1)
            act.wait_ge(columns_landed[0], 2 * 16)
            for i, (which, half) in enumerate(FIRST_ORDER):
                act.wait_ge(x_turned, half + 1)
                first_part(0, which, half_of(half))
            for i in range(3):
                which, half = FIRST_ORDER[i]
                second_part(0, which, i + 1, half_of(half))
            act.wait_ge(x_turned, 2 * B)
            first_part(1, 1)
            first_part(1, 0)
            which, half = FIRST_ORDER[3]
            second_part(0, which, 4, half_of(half))
            act.wait_ge(w_turned, 1)
            nc.scalar.activation(w_T[:, 0:2, :].rearrange("p i c -> p (i c)"), max_ps[:, 1, 1, 0:2 * P], ACT.Identity)\
                .then_inc(w_scaled, 1)
            nc.scalar.activation(w_T[:, 2, :], max_ps[:, 1, 1, 2 * P:3 * P], ACT.Identity, scale=0.5).then_inc(w_scaled, 1)
            second_part(1, 1, ROW1 + 1)
            second_part(1, 0, ROW1 + 2)

            def copy_turned(half, rank):
                nc.scalar.activation(max_turned[:, half, :], ring_ps[0:MAXROWS, slot(rank), 0:P // 2].bitcast(BF16),
                                     ACT.Identity).then_inc(ring_drained, 1)

            def save_sums(n, half):
                act.wait_ge(pv_done, STEPS * n + HS * (half + 1))
                nc.scalar.activation(attn_T[:, n, half * HALF:(half + 1) * HALF], acc_ps, ACT.Identity).then_inc(acc_saved, 1)

            def copy_h(p):
                b, token = PIECES[p][0] // NT, PIECES[p][0] % NT * P
                act.wait_ge(h_turned, p + 1)
                nc.scalar.activation(h_T[:, b, 1 + token:1 + token + PIECES[p][1] * P], mix_bank(p, 0), ACT.Identity)\
                    .then_inc(h_copied, 1)

            def take_gate(p):
                act.wait_ge(r_ready, sum(PIECES[p]) // 2)
                nc.scalar.activation(gate[:, tiles_of(p), :].rearrange("p t c -> p (t c)"), mix_bank(p, 0), ACT.Tanh,
                                     scale=0.5).then_inc(gate_done, 1)

            def normalise_out(p):
                act.wait_ge(z_scale, p + 1)
                for t in act_tiles(p):
                    nc.scalar.activation(o_sb[:, t, :], z_sb[:, t, :], ACT.Identity,
                                         scale=rstd[:, 1, t:t + 1], bias=neg_mean_rstd[:, t:t + 1]).then_inc(o_ready, 1)

            def before_exponential(place):
                if place == 13:
                    copy_h(0)
                elif place == 20:
                    take_gate(0)
                elif place == 25:
                    copy_h(1)
                elif place == 32:
                    take_gate(1)
                elif place == 38:
                    copy_h(2)
                elif place == 45:
                    take_gate(2)

            def group(n, first=False, last=False):
                for s in range(STEPS):
                    if s == TURN1 or (s == TURN0 and not last):
                        half = 1 if s == TURN1 else 0
                        act.wait_ge(ring_filled, turn_rank(n, half) + 1)
                        copy_turned(half, turn_rank(0, half))
                    if not (first and s < 2):
                        act.wait_ge(pv_done, STEPS * n + s - 1)
                    for h in range(GH):
                        u = GH * s + h
                        if last and s >= FREE:
                            before_exponential((s - FREE) * (GH + 1) + h)
                        act.wait_ge(ring_filled, fill_rank(n, u, last) + 1)
                        nc.scalar.activation(probs[:, s % 2, h, :], ring_ps[:, slot(fill_rank(0, u, last)), :], ACT.Exp,
                                             scale=SCALE).then_inc(ring_drained, 1)
                        if s == 1 and h == 0 and not first:
                            save_sums(n - 1, 1)
                        if s == HS + 1 and h == 0:
                            save_sums(n, 0)

            act.wait_ge(ring_filled, 1)
            copy_turned(0, 0)
            group(0, first=True)
            with act.Fori(0, (NG - 2) // BUF) as k:
                for j in range(1, BUF + 1):
                    group(k * BUF + j)
            group(NG - 1, last=True)
            save_sums(NG - 1, 1)

            for p in range(3):
                normalise_out(p)
            copy_h(3)
            copy_h(4)
            take_gate(3)
            take_gate(4)
            normalise_out(3)
            normalise_out(4)

        @block.vector
        def _(dve):
            nc.vector.memset(k_stack[P // 2:P, 0, :, :], 1.0).then_inc(ones_set, 1)
            dve.wait_ge(columns_landed[0], 2 * 16)
            dve.wait_ge(columns_landed[1], 2 * 16)

            def take_rest(b, which, counted, tokens=slice(0, T)):
                dve.wait_ge(first_parts, counted)
                nc.vector.scalar_tensor_tensor(out=qk_rest[:, 2 * b + which, tokens], in0=turned_x(b)[:, tokens],
                                               scalar=columns[:, which:which + 1],
                                               in1=qk_parts[:, 2 * b + which, 0, tokens], op0=ALU.mult, op1=ALU.subtract)\
                    .then_inc(rests_taken, 1)

            def third_part(i):
                which, half = FIRST_ORDER[i]
                tokens = slice(half * HALF, (half + 1) * HALF)
                dve.wait_ge(rests_taken, i + 1)
                dve.wait_ge(second_parts, i + 1)
                nc.vector.tensor_tensor(qk_parts[:, which, 2, tokens], qk_rest[:, which, tokens], qk_parts[:, which, 1, tokens],
                                        ALU.subtract).then_inc(third_parts, 1)

            def first_rest(i):
                which, half = FIRST_ORDER[i]
                take_rest(0, which, 2 * half + 2, slice(half * HALF, (half + 1) * HALF))

            for i in range(3):
                first_rest(i)
            for i in range(3):
                third_part(i)
            first_rest(3)
            third_part(3)
            for which in (1, 0):
                take_rest(1, which, ROW1 + 2)

            def take_max(n, e):
                tile, h = e // GH, e % GH
                column = h * (NT // 2) + tile % (NT // 2)
                dve.wait_ge(rows_ready, GUNITS * n + e + 1)
                nc.vector.tensor_reduce(neg_max[:, tile // (NT // 2), column:column + 1],
                                        max_ps[:, e % 2, :, :].rearrange("p k t -> p (k t)"), AX.X, ALU.max,
                                        negate=True).then_inc(max_taken, 1)

            with dve.Fori(0, NG) as n:
                for e in range(GUNITS):
                    take_max(n, e)

            links = [0]

            def link(ins):
                links[0] += 1
                ins.then_inc(dve_linked, 1)
                dve.wait_ge(dve_linked, links[0])

            def scale_attention(unit):
                tiles = slice(2 * unit, 2 * unit + 2)
                heads = turn_banks(unit).rearrange("p t (h w) -> p t h w", w=VW)
                dve.wait_ge(attn_turned, 2 * (unit + 1))
                nc.vector.reciprocal(recip_sum[:, tiles, :], heads[:, :, :, D]).then_inc(sums_inverted, 1)
                dve.wait_ge(sums_inverted, unit + 1)
                nc.vector.tensor_tensor(y_sb[:, tiles, :].rearrange("p t (h d) -> p t h d", d=D), heads[:, :, :, 0:D],
                                        recip_sum[:, tiles, :].unsqueeze(3).to_broadcast([P, 2, H, D]), ALU.mult)\
                    .then_inc(attn_scaled, 1)

            def last_attention(heads):
                tiles, channels = slice(PIECES[3][0], B * NT), slice(heads[0] * D, (heads[-1] + 1) * D)
                sums = max_ps[:, :, :, :].rearrange("p a t (h w) -> p (a t) h w", w=VW)[:, :, heads[0]:heads[-1] + 1, :]
                recip = recip_sum[:, tiles, heads[0]:heads[-1] + 1]
                y = y_sb[:, tiles, channels]
                if heads[0] == 0:
                    dve.wait_ge(early_turned, 4)
                else:
                    dve.wait_ge(attn_turned, B * NT)
                link(nc.vector.reciprocal(recip, sums[:, :, :, D]))
                link(nc.vector.tensor_tensor(y.rearrange("p t (h d) -> p t h d", d=D), sums[:, :, :, 0:D],
                                             recip.unsqueeze(3).to_broadcast([P, 4, len(heads), D]), ALU.mult))
                added = nc.vector.tensor_tensor(y, y, x_sb[:, tiles, channels], ALU.add)
                if heads[0] == 0:
                    added.then_inc(early_scaled, 1)
                    dve.wait_ge(early_scaled, 1)
                else:
                    link(added)

            def average(norm, *pieces):
                for p in pieces:
                    dve.wait_ge(stats_taken[norm], sum(PIECES[p]))
                    for t in range(PIECES[p][0], sum(PIECES[p])):
                        nc.vector.bn_aggr(mean_var[:, norm, t, :], stats[:, norm, t, :]).then_inc(averaged[norm], 1)
                for p in pieces:
                    dve.wait_ge(averaged[norm], sum(PIECES[p]))
                    nc.vector.tensor_scalar(var_eps[:, norm, tiles_of(p)], mean_var[:, norm, tiles_of(p), 1], EPS, None, ALU.add)\
                        .then_inc(eps_added[norm], 1)

            def add_x(*units):
                for unit in units:
                    y = y_sb[:, 2 * unit:2 * unit + 2, :]
                    dve.wait_ge(attn_scaled, unit + 1)
                    nc.vector.tensor_tensor(y, y, x_sb[:, 2 * unit:2 * unit + 2, :], ALU.add).then_inc(x_added, 1)
                for unit in units:
                    dve.wait_ge(x_added, unit + 1)
                    for t in range(2 * unit, 2 * unit + 2):
                        nc.vector.bn_stats(stats[:, 0, t, :], y_sb[:, t, :]).then_inc(stats_taken[0], 1)

            def norm_h(p):
                dve.wait_ge(rstd_ready[0], p + 1)
                for t in range(PIECES[p][0], sum(PIECES[p])):
                    nc.vector.tensor_scalar(h_sb[:, t, :], y_sb[:, t, :], mean_var[:, 0, t, 0:1],
                                            rstd[:, 0, t:t + 1], ALU.subtract, ALU.mult).then_inc(h_ready, 1)

            def mix_for(p, i):
                b, token, first, count = PIECES[p][0] // NT, PIECES[p][0] % NT * P, PIECES[p][0] * P, PIECES[p][1] * P
                before, now = h_T[:, b, token:token + count], h_T[:, b, 1 + token:1 + token + count]
                if i == 1:
                    dve.wait_ge(h_copied, p + 1)
                    if p == 0:
                        dve.wait_ge(tail_set, 2)
                    link(nc.vector.tensor_tensor(change[:, first:first + count], now, before, ALU.subtract))
                nc.vector.scalar_tensor_tensor(out=mixed[:, i, first:first + count], in0=change[:, first:first + count],
                                               scalar=columns[:, 2 + i:3 + i], in1=before, op0=ALU.mult, op1=ALU.add)\
                    .then_inc((r_mixed, k_mixed)[i], 1)

            def square_k(p):
                first = PIECES[p][0] * P
                dve.wait_ge(k_ready, p + 1)
                k = k_act[:, first:first + PIECES[p][1] * P]
                link(nc.vector.tensor_scalar(k, mix_bank(p, 1), 0.0, None, ALU.max))
                nc.vector.tensor_tensor(k, k, k, ALU.mult).then_inc(k_act_done, 1)

            def apply_gate(p):
                z = z_sb[:, tiles_of(p), :]
                dve.wait_ge(v_ready, sum(PIECES[p]) // 2)
                dve.wait_ge(gate_done, p + 1)
                nc.vector.scalar_tensor_tensor(out=z.rearrange("p t c -> p (t c)"),
                                               in0=gate[:, tiles_of(p), :].rearrange("p t c -> p (t c)"), scalar=1.0,
                                               in1=mix_bank(p, 1), op0=ALU.add, op1=ALU.mult).then_inc(gated, 1)

            def z_stats(p):
                z = z_sb[:, tiles_of(p), :]
                if p >= 3:
                    dve.wait_ge(gated, p + 1)
                    dve.wait_ge(h_ready, sum(PIECES[p]))
                    link(nc.vector.tensor_tensor(z, z, h_sb[:, tiles_of(p), :], ALU.add))
                else:
                    dve.wait_ge(h_added, p + 1)
                for t in range(PIECES[p][0], sum(PIECES[p])):
                    nc.vector.bn_stats(stats[:, 1, t, :], z_sb[:, t, :]).then_inc(stats_taken[1], 1)
                average(1, p)

            def z_bias(p):
                dve.wait_ge(rstd_ready[1], p + 1)
                nc.vector.scalar_tensor_tensor(out=neg_mean_rstd[:, tiles_of(p)], in0=mean_var[:, 1, tiles_of(p), 0], scalar=-1.0,
                                               in1=rstd[:, 1, tiles_of(p)], op0=ALU.mult, op1=ALU.mult).then_inc(z_scale, 1)

            def normalise_out(p):
                t = PIECES[p][0] + 1
                nc.vector.tensor_scalar(o_sb[:, t, :], z_sb[:, t, :], mean_var[:, 1, t, 0:1],
                                        rstd[:, 1, t:t + 1], ALU.subtract, ALU.mult).then_inc(dve_o_ready, 1)

            scale_attention(0)
            add_x(0)
            scale_attention(1)
            add_x(1)
            average(0, 0)
            scale_attention(2)
            scale_attention(3)
            norm_h(0)
            add_x(2, 3)
            mix_for(0, 1)
            mix_for(0, 0)
            average(0, 1)
            square_k(0)
            norm_h(1)
            apply_gate(0)
            scale_attention(4)
            add_x(4)
            mix_for(1, 1)
            mix_for(1, 0)
            scale_attention(5)
            add_x(5)
            average(0, 2)
            square_k(1)
            norm_h(2)
            apply_gate(1)
            mix_for(2, 1)
            mix_for(2, 0)
            z_stats(0)
            square_k(2)
            z_stats(1)
            apply_gate(2)
            z_bias(0)
            z_bias(1)
            z_stats(2)
            last_attention(range(0, H - GH))
            last_attention(range(H - GH, H))
            for t in range(PIECES[3][0], B * NT):
                nc.vector.bn_stats(stats[:, 0, t, :], y_sb[:, t, :]).then_inc(stats_taken[0], 1)
            average(0, 3, 4)
            z_bias(2)
            norm_h(3)
            norm_h(4)
            mix_for(3, 1)
            mix_for(4, 1)
            mix_for(3, 0)
            square_k(3)
            mix_for(4, 0)
            square_k(4)
            apply_gate(3)
            z_stats(3)
            apply_gate(4)
            z_stats(4)
            z_bias(3)
            normalise_out(3)
            z_bias(4)
            normalise_out(4)

        @block.gpsimd
        def _(pool):
            nc.gpsimd.memset(ident[:, :], 0.0).then_inc(ident_steps, 1)
            nc.gpsimd.memset(ident_bf[:, :], 0.0).then_inc(ident_steps, 1)
            pool.wait_ge(ident_steps, 2)
            for m in (ident, ident_bf):
                nc.gpsimd.affine_select(out=m[:, :], in_=m[:, :], compare_op=ALU.not_equal, fill=1.0, base=0,
                                        pattern=[[-1, P]], channel_multiplier=1).then_inc(ident_set, 1)
            pool.wait_ge(ident_set, 2)
            for buf in range(BUF):
                nc.gpsimd.memset(q_stack[P // 2:P, buf].rearrange("p k h t -> p (k h t)").bitcast(F32), 0.0).then_inc(pool_rows_set, 1)
                if buf > 0:
                    nc.gpsimd.memset(k_stack[P // 2:P, buf, :, :], 1.0).then_inc(pool_rows_set, 1)
            pool.wait_ge(pool_rows_set, 2 * BUF - 1)
            nc.gpsimd.memset(max_parts[:, :, :, :], 0.0).then_inc(v_cleared, 1)
            nc.gpsimd.memset(no_max[:, :], 0.0).then_inc(v_cleared, 1)
            nc.gpsimd.memset(v_aug[:, :, :, :, :], 0.0).then_inc(v_cleared, 1)
            pool.wait_ge(v_cleared, 3)
            nc.gpsimd.memset(v_aug[:, :, :, :, D:D + 1], 1.0).then_inc(v_cleared, 1)
            pool.wait_ge(v_cleared, 4)

            def stage_v(n, buf):
                src = x_sb[:, :, :].rearrange("p (b t) (g c) -> p b t g c", b=B, g=GPB)[:, n // GPB, :, n % GPB, :]
                nc.gpsimd.tensor_copy(v_aug[:, buf, :, :, 0:D], src.rearrange("p t (h d) -> p t h d", d=D)).then_inc(v_staged, 1)

            def split_max(n, half):
                done = 8 * n + 4 * half
                pool.wait_ge(max_taken, GUNITS * n + GUNITS // 2 * (half + 1))
                nc.gpsimd.tensor_tensor(max_parts[:, half, 0, :], neg_max[:, half, :], no_max[:, :], ALU.add).then_inc(max_split, 1)
                pool.wait_ge(max_split, done + 1)
                nc.gpsimd.tensor_tensor(max_rest[:, half, 0, :], neg_max[:, half, :], max_parts[:, half, 0, :], ALU.subtract)\
                    .then_inc(max_split, 1)
                pool.wait_ge(max_split, done + 2)
                nc.gpsimd.tensor_tensor(max_parts[:, half, 1, :], max_rest[:, half, 0, :], no_max[:, :], ALU.add).then_inc(max_split, 1)
                pool.wait_ge(max_split, done + 3)
                nc.gpsimd.tensor_tensor(max_parts[:, half, 2, :], max_rest[:, half, 0, :], max_parts[:, half, 1, :], ALU.subtract)\
                    .then_inc(max_split, 1)

            for i in range(NC):
                pool.wait_ge(x_landed[i], 16)
            stage_v(0, 0)
            for i, which in enumerate((1, 0)):
                pool.wait_ge(second_parts, ROW1 + i + 1)
                pool.wait_ge(rests_taken, ROW1 + i + 1)
                nc.gpsimd.tensor_tensor(qk_parts[:, 2 + which, 2, :], qk_rest[:, 2 + which, :], qk_parts[:, 2 + which, 1, :],
                                        ALU.subtract).then_inc(pool_third_parts, 1)

            split_max(0, 0)

            def group(n, j):
                split_max(n, 1)
                stage_v(n + 1, (j + 1) % BUF)
                split_max(n + 1, 0)

            with pool.Fori(0, (NG - 2) // BUF) as k:
                for j in range(BUF):
                    group(k * BUF + j, j)
            group(NG - 2, (NG - 2) % BUF)
            split_max(NG - 1, 1)

            nc.gpsimd.memset(h_T[:, :, 0:1], 0.0).then_inc(tail_set, 1)
            nc.gpsimd.memset(minus_half[:, :], -0.5).then_inc(tail_set, 1)
            pool.wait_ge(tail_set, 2)

            def take_rstd(norm, p):
                pool.wait_ge(eps_added[norm], p + 1)
                nc.gpsimd.tensor_tensor(rstd[:, norm, tiles_of(p)], var_eps[:, norm, tiles_of(p)],
                                        minus_half[:, 0:PIECES[p][1]], ALU.pow).then_inc(rstd_ready[norm], 1)

            def add_h(p):
                pool.wait_ge(gated, p + 1)
                pool.wait_ge(h_ready, sum(PIECES[p]))
                z = z_sb[:, tiles_of(p), :]
                nc.gpsimd.tensor_tensor(z, z, h_sb[:, tiles_of(p), :], ALU.add).then_inc(h_added, 1)

            take_rstd(0, 0)
            take_rstd(0, 1)
            add_h(0)
            take_rstd(0, 2)
            add_h(1)
            take_rstd(1, 0)
            take_rstd(1, 1)
            add_h(2)
            take_rstd(1, 2)
            take_rstd(0, 3)
            take_rstd(0, 4)
            take_rstd(1, 3)
            take_rstd(1, 4)


_INS = ["L0_attn_inputs", "L0_attn_rotation_params", "L0_attn_entangle_params", "L0_ffn_W_r", "L0_ffn_W_k",
        "L0_ffn_W_v", "L0_ffn_mu_r", "L0_ffn_mu_k"]


def kernel(**inputs):
    import numpy as _np
    import concourse.bacc as _bacc
    from concourse import mybir as _mybir
    from concourse.bass_utils import run_bass_kernel_spmd as _run

    nc = _bacc.Bacc("TRN2", target_bir_lowering=False, num_devices=1)
    arrays, args = {}, []
    for name in _INS:
        a = _np.ascontiguousarray(inputs[name])
        arrays[f"in_{name}_dram"] = a
        args.append(nc.dram_tensor(f"in_{name}_dram", a.shape, _mybir.dt.from_np(a.dtype), kind="ExternalInput").ap())
    shape = inputs["L0_attn_inputs"].shape
    args.append(nc.dram_tensor("out_dram", shape, _mybir.dt.float32, kind="ExternalOutput").ap())
    build_attention_ffn(nc, *args)
    r = _run(nc, [arrays], core_ids=[0])
    return r.results[0]["out_dram"]
```
